# Optimizing a Trainium2 kernel written in Bass

```python
import numpy as np
import jax
import jax.numpy as jnp

def _softmax(x, axis=-1):
    return jax.nn.softmax(x, axis=axis)

def _gelu(x):
    return jax.nn.gelu(x, approximate=True)

def _silu(x):
    return jax.nn.silu(x)

def _sigmoid(x):
    return jax.nn.sigmoid(x)

def _layernorm(x, axis=-1, eps=1e-05):
    m = jnp.mean(x, axis=axis, keepdims=True)
    v = jnp.var(x, axis=axis, keepdims=True)
    return (x - m) / jnp.sqrt(v + eps)

def _scatter_add(tgt, idx, src, axis=0):
    return tgt.at[idx].add(src)

def _segment_sum(src, seg, n):
    return jax.ops.segment_sum(src, seg, n)
kernel_name = 'mk_lm_tower_d1_tok_ids512_r4_48e948'

def setup_inputs(seed: int=0):
    np.random.seed(seed)
    _w = jnp.asarray

    def _rec_inputs():
        import jax
        import jax.numpy as jnp
        _rk = jax.random.key(seed)
        x = jax.random.randint(jax.random.fold_in(_rk, 1), (16, 512), 0, 16, jnp.int32)
        return x
    x = _rec_inputs()

    def _L0_tok_setup():
        import jax, jax.numpy as jnp
        import numpy as np
        VOCAB = 16
        D_MODEL = 128
        D_EMB = int(D_MODEL * 0.7)
        D_STFT = D_MODEL - D_EMB
        N_FFT = 64
        HOP = 64
        N_FREQ = N_FFT // 2 + 1
        B, L = (4, 2048)

        def _stft_mag(signal):
            pad = N_FFT // 2
            padded = jnp.pad(signal, ((0, 0), (pad, pad)), mode='reflect')
            n_frames = signal.shape[1] // HOP + 1
            idx = jnp.arange(n_frames)[:, None] * HOP + jnp.arange(N_FFT)[None, :]
            window = 0.5 - 0.5 * jnp.cos(2.0 * jnp.pi * jnp.arange(N_FFT) / N_FFT)
            frames = padded[:, idx] * window.astype(signal.dtype)
            return jnp.abs(jnp.fft.rfft(frames, axis=-1))
        key = jax.random.key(seed)
        k1, k2, k3, k4 = jax.random.split(key, 4)
        input_ids = jax.random.randint(k1, (B, L), 0, VOCAB)
        emb_table = jax.random.normal(k2, (VOCAB, D_EMB), dtype=jnp.float32) * 0.02
        proj_w = jax.random.normal(k3, (VOCAB * N_FREQ, D_STFT), dtype=jnp.float32) * 0.02
        proj_b = jnp.zeros((D_STFT,), dtype=jnp.float32)
        return {'input_ids': input_ids, 'emb_table': emb_table, 'proj_w': proj_w, 'proj_b': proj_b}
    _L0_tok_all = _L0_tok_setup()
    _L0_tok_in = {k: v for k, v in _L0_tok_all.items() if k in ('emb_table', 'proj_w', 'proj_b')}
    del _L0_tok_all

    def _L0_attn_setup():
        import jax, jax.numpy as jnp
        import numpy as np
        EMBED_DIM = 128
        NUM_HEADS = 8
        HEAD_DIM = EMBED_DIM // NUM_HEADS
        LOCAL_SIZE = 17
        NUM_WTOK = 64
        SCALING = float(HEAD_DIM) ** (-0.5)

        def get_overlap_segments(x, window_size):
            if window_size % 2 == 0:
                window_size += 1
            pad = (window_size - 1) // 2
            xp = jnp.pad(x, ((0, 0), (pad, pad), (0, 0)))
            idx = jnp.arange(x.shape[1])[:, None] + jnp.arange(window_size)[None, :]
            return xp[:, idx, :]
        key = jax.random.key(seed)
        k = jax.random.split(key, 5)
        B, T, E = (2, NUM_WTOK + 1024, EMBED_DIM)
        s = 1.0 / np.sqrt(E).astype(np.float32)
        return {'x': jax.random.normal(k[0], (B, T, E), jnp.float32), 'W_qkv': jax.random.normal(k[1], (E, 3 * E), jnp.float32) * s, 'b_qkv': jax.random.normal(k[2], (3 * E,), jnp.float32) * 0.01, 'W_out': jax.random.normal(k[3], (E, E), jnp.float32) * s, 'b_out': jax.random.normal(k[4], (E,), jnp.float32) * 0.01}
    _L0_attn_all = _L0_attn_setup()
    _L0_attn_in = {k: v for k, v in _L0_attn_all.items() if k in ('W_qkv', 'b_qkv', 'W_out', 'b_out')}
    del _L0_attn_all

    def _L0_ffn_setup():
        import jax, jax.numpy as jnp
        import numpy as np
        S, B, I, O, H, E, K = (128, 32, 128, 128, 128, 8, 2)

        def _expert(x_seq, Wi, Wh, b, Wo, bo):
            Bsz = x_seq.shape[1]
            Hd = Wh.shape[0]

            def step(carry, xt):
                h, c = carry
                gates = xt @ Wi + h @ Wh + b
                i_, f_, g_, o_ = jnp.split(gates, 4, axis=-1)
                c = jax.nn.sigmoid(f_) * c + jax.nn.sigmoid(i_) * jnp.tanh(g_)
                h = jax.nn.sigmoid(o_) * jnp.tanh(c)
                return ((h, c), h @ Wo + bo)
            init = (jnp.zeros((Bsz, Hd), x_seq.dtype), jnp.zeros((Bsz, Hd), x_seq.dtype))
            _, ys = jax.lax.scan(step, init, x_seq)
            return ys
        key = jax.random.key(seed)
        ks = jax.random.split(key, 6)
        s = 0.02
        return {'x': jax.random.normal(ks[0], (S, B, I), dtype=jnp.float32), 'router_w': jax.random.normal(ks[1], (I, E), dtype=jnp.float32) * s, 'router_b': jnp.zeros((E,), dtype=jnp.float32), 'Wi': jax.random.normal(ks[2], (E, I, 4 * H), dtype=jnp.float32) * s, 'Wh': jax.random.normal(ks[3], (E, H, 4 * H), dtype=jnp.float32) * s, 'b': jnp.zeros((E, 4 * H), dtype=jnp.float32), 'Wo': jax.random.normal(ks[4], (E, H, O), dtype=jnp.float32) * s, 'bo': jnp.zeros((E, O), dtype=jnp.float32)}
    _L0_ffn_all = _L0_ffn_setup()
    _L0_ffn_in = {k: v for k, v in _L0_ffn_all.items() if k in ('router_w', 'router_b', 'Wi', 'Wh', 'b', 'Wo', 'bo')}
    del _L0_ffn_all
    return {'x': x, 'L0_tok_emb_table': _L0_tok_in['emb_table'], 'L0_tok_proj_w': _L0_tok_in['proj_w'], 'L0_tok_proj_b': _L0_tok_in['proj_b'], 'L0_attn_W_qkv': _L0_attn_in['W_qkv'], 'L0_attn_b_qkv': _L0_attn_in['b_qkv'], 'L0_attn_W_out': _L0_attn_in['W_out'], 'L0_attn_b_out': _L0_attn_in['b_out'], 'L0_ffn_router_w': _L0_ffn_in['router_w'], 'L0_ffn_router_b': _L0_ffn_in['router_b'], 'L0_ffn_Wi': _L0_ffn_in['Wi'], 'L0_ffn_Wh': _L0_ffn_in['Wh'], 'L0_ffn_b': _L0_ffn_in['b'], 'L0_ffn_Wo': _L0_ffn_in['Wo'], 'L0_ffn_bo': _L0_ffn_in['bo']}

def reference(x, L0_tok_emb_table, L0_tok_proj_w, L0_tok_proj_b, L0_attn_W_qkv, L0_attn_b_qkv, L0_attn_W_out, L0_attn_b_out, L0_ffn_router_w, L0_ffn_router_b, L0_ffn_Wi, L0_ffn_Wh, L0_ffn_b, L0_ffn_Wo, L0_ffn_bo):
    import jax
    import jax.numpy as jnp

    def _L0_tok_ref(input_ids, emb_table, proj_w, proj_b):
        import jax, jax.numpy as jnp
        import numpy as np
        VOCAB = 16
        D_MODEL = 128
        D_EMB = int(D_MODEL * 0.7)
        D_STFT = D_MODEL - D_EMB
        N_FFT = 64
        HOP = 64
        N_FREQ = N_FFT // 2 + 1
        B, L = (4, 2048)

        def _stft_mag(signal):
            pad = N_FFT // 2
            padded = jnp.pad(signal, ((0, 0), (pad, pad)), mode='reflect')
            n_frames = signal.shape[1] // HOP + 1
            idx = jnp.arange(n_frames)[:, None] * HOP + jnp.arange(N_FFT)[None, :]
            window = 0.5 - 0.5 * jnp.cos(2.0 * jnp.pi * jnp.arange(N_FFT) / N_FFT)
            frames = padded[:, idx] * window.astype(signal.dtype)
            return jnp.abs(jnp.fft.rfft(frames, axis=-1))
        b, seq_len = input_ids.shape
        word_embeds = emb_table[input_ids]
        onehot = jax.nn.one_hot(input_ids, VOCAB, dtype=jnp.float32)
        signal = onehot.transpose(0, 2, 1).reshape(b * VOCAB, seq_len)
        spec = _stft_mag(signal)
        n_frames = spec.shape[1]
        stft_mag = spec.reshape(b, VOCAB, n_frames, N_FREQ).transpose(0, 1, 3, 2)
        stft_to_up = stft_mag.transpose(0, 2, 1, 3).reshape(b, N_FREQ * VOCAB, n_frames)
        up_idx = jnp.arange(seq_len) * n_frames // seq_len
        stft_up = stft_to_up[:, :, up_idx]
        feats = stft_up.transpose(0, 2, 1)
        stft_enc = jnp.einsum('bli,io->blo', feats, proj_w) + proj_b
        return jnp.concatenate([word_embeds, stft_enc], axis=-1)

    def _L0_attn_ref(x, W_qkv, b_qkv, W_out, b_out):
        import jax, jax.numpy as jnp
        import numpy as np
        EMBED_DIM = 128
        NUM_HEADS = 8
        HEAD_DIM = EMBED_DIM // NUM_HEADS
        LOCAL_SIZE = 17
        NUM_WTOK = 64
        SCALING = float(HEAD_DIM) ** (-0.5)

        def get_overlap_segments(x, window_size):
            if window_size % 2 == 0:
                window_size += 1
            pad = (window_size - 1) // 2
            xp = jnp.pad(x, ((0, 0), (pad, pad), (0, 0)))
            idx = jnp.arange(x.shape[1])[:, None] + jnp.arange(window_size)[None, :]
            return xp[:, idx, :]
        b, t, E = x.shape
        H, Dh, NW = (NUM_HEADS, HEAD_DIM, NUM_WTOK)
        BH = b * H
        qkv = x @ W_qkv + b_qkv
        Q, K, V = jnp.split(qkv, 3, axis=-1)
        Q = Q * SCALING

        def heads(z):
            return z.reshape(b, t, H, Dh).transpose(0, 2, 1, 3).reshape(BH, t, Dh)
        Q, K, V = (heads(Q), heads(K), heads(V))
        Qw, Qf = (Q[:, :NW], Q[:, NW:])
        Kw, Kf = (K[:, :NW], K[:, NW:])
        Vw, Vf = (V[:, :NW], V[:, NW:])
        t_fea = t - NW
        pad_len = (NW - t_fea % NW) % NW
        Kp = jnp.pad(Kf, ((0, 0), (0, pad_len), (0, 0)))
        Vp = jnp.pad(Vf, ((0, 0), (0, pad_len), (0, 0)))
        chunk = (t_fea + pad_len) // NW
        Kp = Kp.reshape(BH, NW, chunk, Dh)
        Vp = Vp.reshape(BH, NW, chunk, Dh)
        Kcat = jnp.concatenate([Kw[:, :, None, :], Kp], axis=2)
        Vcat = jnp.concatenate([Vw[:, :, None, :], Vp], axis=2)
        aw = jax.nn.softmax(jnp.einsum('bnd,bncd->bnc', Qw, Kcat), axis=-1)
        out_wtok = jnp.einsum('bnc,bncd->bnd', aw, Vcat)
        out_wtok_expa = jnp.repeat(out_wtok, chunk, axis=1)[:, :t_fea]
        Kseg = get_overlap_segments(Kf, LOCAL_SIZE)
        Vseg = get_overlap_segments(Vf, LOCAL_SIZE)
        Kfull = jnp.concatenate([out_wtok_expa[:, :, None, :], Kseg], axis=2)
        scores = jnp.einsum('btd,btwd->btw', Qf, Kfull)
        w_wtok = scores[:, :, 0]
        w_wtok = jnp.pad(w_wtok, ((0, 0), (0, pad_len)), constant_values=-jnp.inf)
        w_wtok = jax.nn.softmax(w_wtok.reshape(BH, NW, chunk), axis=-1)
        w_wtok = w_wtok.reshape(BH, NW * chunk)[:, :t_fea, None]
        w_fea = jax.nn.softmax(scores[:, :, 1:], axis=-1)
        attn = jnp.concatenate([w_wtok, w_fea], axis=-1)
        Vfull = jnp.concatenate([out_wtok_expa[:, :, None, :], Vseg], axis=2)
        out_fea = jnp.einsum('btw,btwd->btd', attn, Vfull)
        out = jnp.concatenate([out_wtok, out_fea], axis=1)
        out = out.reshape(b, H, t, Dh).transpose(0, 2, 1, 3).reshape(b, t, E)
        return out @ W_out + b_out

    def _L0_ffn_ref(x, router_w, router_b, Wi, Wh, b, Wo, bo):
        import jax, jax.numpy as jnp
        import numpy as np
        S, B, I, O, H, E, K = (128, 32, 128, 128, 128, 8, 2)

        def _expert(x_seq, Wi, Wh, b, Wo, bo):
            Bsz = x_seq.shape[1]
            Hd = Wh.shape[0]

            def step(carry, xt):
                h, c = carry
                gates = xt @ Wi + h @ Wh + b
                i_, f_, g_, o_ = jnp.split(gates, 4, axis=-1)
                c = jax.nn.sigmoid(f_) * c + jax.nn.sigmoid(i_) * jnp.tanh(g_)
                h = jax.nn.sigmoid(o_) * jnp.tanh(c)
                return ((h, c), h @ Wo + bo)
            init = (jnp.zeros((Bsz, Hd), x_seq.dtype), jnp.zeros((Bsz, Hd), x_seq.dtype))
            _, ys = jax.lax.scan(step, init, x_seq)
            return ys
        S_, B_, I_ = x.shape
        N = S_ * B_
        flat_x = x.reshape(N, I_)
        logits = flat_x @ router_w + router_b
        top_vals, top_idx = jax.lax.top_k(logits, K)
        rw = jax.nn.softmax(top_vals, axis=1)
        mask = (top_idx.T[:, None, :] == jnp.arange(E)[None, :, None]).astype(x.dtype)
        expert_x = (mask[..., None] * flat_x[None, None]).reshape(K, E, S_, B_, I_)
        run_e = jax.vmap(_expert, in_axes=(0, 0, 0, 0, 0, 0))
        run_ke = jax.vmap(run_e, in_axes=(0, None, None, None, None, None))
        out = run_ke(expert_x, Wi, Wh, b, Wo, bo)
        out = out.reshape(K, E, N, -1)
        y = jnp.einsum('ken,nk,keno->no', mask, rw, out)
        return y.reshape(S_, B_, -1)
    h = _L0_tok_ref(x, L0_tok_emb_table, L0_tok_proj_w, L0_tok_proj_b)
    h = h + _L0_attn_ref(_layernorm(h, axis=-1), L0_attn_W_qkv, L0_attn_b_qkv, L0_attn_W_out, L0_attn_b_out)
    h = h + _L0_ffn_ref(_layernorm(h, axis=-1), L0_ffn_router_w, L0_ffn_router_b, L0_ffn_Wi, L0_ffn_Wh, L0_ffn_b, L0_ffn_Wo, L0_ffn_bo)
    return h

_drawn_inputs = setup_inputs


def setup_inputs(seed=0):
    import zlib

    import numpy as np

    out = dict(_drawn_inputs(seed))
    spreads = {'L0_tok_proj_b': (0.0, 0.1),
     'L0_ffn_router_b': (0.0, 0.1),
     'L0_ffn_b': (0.0, 0.8),
     'L0_ffn_bo': (0.0, 0.1)}
    factors = {'L0_attn_b_qkv': 4.316,
     'L0_attn_b_out': 4.936,
     'L0_ffn_Wi': 5.078,
     'L0_ffn_Wh': 8.0,
     'L0_ffn_Wo': 4.933}
    for name, (base, spread) in spreads.items():
        noise = np.random.default_rng([zlib.crc32(name.encode()), seed]).standard_normal(out[name].shape)
        drawn = base * np.exp(spread * noise) if base else spread * noise
        out[name] = jnp.asarray(drawn.astype(out[name].dtype))
    for name, factor in factors.items():
        out[name] = (out[name] * factor).astype(out[name].dtype)
    return out
```

```python
import concourse.bass as bass
from concourse import mybir
from contextlib import ExitStack


def lm_tower_kernel(nc, x_ids, frame_ids, emb_table, proj_w, proj_b, w_qkv, b_qkv, w_out, b_out,
                    router_w, router_b, wi, wh, b_lstm, wo, bo,
                    dft, vocab_col, vocab_rows, frame_rows, ident_dram, head_ones, band, parity, expert_m8, out):
    f32, f16, bf16, i32 = mybir.dt.float32, mybir.dt.float16, mybir.dt.bfloat16, mybir.dt.int32
    ALU = mybir.AluOpType
    ACT = mybir.ActivationFunctionType
    X = mybir.AxisListType.X

    P = 128
    STEPS, SEQ = x_ids.shape
    VOCAB, D_EMB = 16, 89
    D = w_out.shape[0]
    D_ENC = D - D_EMB
    NFFT, NFREQ = dft.shape[0], dft.shape[2]
    NFR = SEQ // NFFT + 1
    HEADS, DH = 8, 16
    NW = 64
    TF = SEQ - NW
    CH = TF // NW
    PAD = 8
    QB = 16
    KB = QB + 2 * PAD
    NBLK = TF // QB
    HB = NBLK // 2
    E = wi.shape[0]
    K = 2
    TILES = SEQ // P
    EPS = 1e-5
    W_SCALE, V_SCALE = 2.0 ** 6, 2.0 ** 8
    UNSCALE = 1.0 / (W_SCALE * V_SCALE)
    I, F, G, O = 0, 1, 2, 3
    ORDER = (I, G, F, O)
    HI, LO = 0, 1
    NG = 4
    ENC0 = 32

    ctx = ExitStack()
    with ctx:
        def sb(name, shape, dt=f32):
            return ctx.enter_context(nc.sbuf_tensor(name, shape, dt))

        def pb(name, shape, dt=f32):
            return ctx.enter_context(nc.psum_tensor(name, shape, dt))

        def sem(name):
            return ctx.enter_context(nc.semaphore(name))

        wi_sb = sb("wi_sb", [P, E, 2, 4 * P], f16)
        wh_sb = sb("wh_sb", [P, E, 2, 4 * P], f16)
        wo_sb = sb("wo_sb", [P, E, 2, P], f16)
        bias_sb = sb("bias_sb", [P, E, 4])
        C = sb("C", [P, E, K * SEQ])
        Hs = sb("Hs", [P, E, 2, K * SEQ], f16)
        tmp = sb("tmp", [P, 5, K * SEQ])
        masks = sb("masks", [P, 2, K, SEQ], f16)
        xm = sb("xm", [P, 2, K, 2, SEQ], f16)
        xs = sb("xs", [P, 2, 2, SEQ], f16)
        h2 = sb("h2", [P, 2, TILES, D])
        wy = sb("wy", [P, 2, TILES, K, E])
        ids = sb("ids", [VOCAB, SEQ], i32)
        rows = sb("rows", [ENC0 + NFR, SEQ])
        table = sb("table", [ENC0 + NFR, D])
        h_sb = sb("h_sb", [P, TILES, D])
        stats = sb("stats", [P, TILES, 6])
        mv = sb("mv", [P, TILES, 2])
        veps = sb("veps", [P, TILES])
        spare = sb("spare", [P, 1])
        rstd = sb("rstd", [P, TILES])
        xn = sb("xn", [P, TILES, D])
        xnT = sb("xnT", [P, SEQ])
        qT = sb("qT", [P, SEQ])
        kw = sb("kw", [P, NW])
        kf = sb("kf", [P, TF + 2 * PAD])
        vw = sb("vw", [P, NW])
        vf = sb("vf", [P, TF + 2 * PAD])
        prod = sb("prod", [P, NW * (CH + 1)])
        ew = sb("ew", [P, NW * (CH + 1)])
        red = sb("red", [P, NW])
        red2 = sb("red2", [P, NW])
        red3 = sb("red3", [P, NW])
        oW = sb("oW", [P, NW])
        qbd = sb("qbd", [P, HEADS * TF])
        vz = sb("vz", [P, P * NBLK])
        vwin = sb("vwin", [P, NBLK * 32])
        pr = sb("pr", [P, NBLK * KB])
        prT = vwin
        wred = sb("wred", [P, 3, NBLK])
        attn = sb("attn", [P, SEQ])
        x32 = xnT
        lg = sb("lg", [P, 8, TILES, E])
        m4 = sb("m4", [P, 10, TILES])
        mk = sb("mk", [P, TILES, K * E])
        mw = sb("mw", [P, TILES, E])
        mrow = ew[0:K * E, 0:SEQ // 2].bitcast(f16)
        wT = attn[0:E, :]
        qperm = attn[:, 0:TF]
        wqkv_sb = sb("wqkv_sb", [P, 3 * D])
        bqkv_sb = sb("bqkv_sb", [P, 3])
        wout_sb = sb("wout_sb", [P, D])
        rw_sb = sb("rw_sb", [P, E])
        rb_sb = sb("rb_sb", [P, E])
        bo_sb = sb("bo_sb", [E, D])
        bout_sb = sb("bout_sb", [1, D])
        ones1 = sb("ones1", [1, P])
        ident = sb("ident", [P, P])
        identb = sb("identb", [P, P], bf16)
        hones = sb("hones", [P, P])
        band_sb = sb("band_sb", [P, KB], f32)
        bandb = sb("bandb", [P, KB], bf16)
        par_sb = sb("par_sb", [P, 2])
        m8_sb = sb("m8_sb", [P, E])
        vcol = sb("vcol", [VOCAB, 1])
        mhalf = sb("mhalf", [P, TILES])

        gates = pb("gates", [P, 2, K * SEQ])
        yp = pb("yp", [P, TILES, D])
        FB = pb("FB", [P, SEQ])
        FA = pb("FA", [P, 2, SEQ])

        stage = C[:, :, :]
        wi_st, wh_st = stage[:, 0:4, :], stage[:, 4:8, :]
        wo_st = xm[:, 0, :, :, :].rearrange("p k v t -> p (k v t)").bitcast(f32)
        NBJ = STEPS * NFR
        fid = tmp[0:NFFT, 1, 0:NBJ].bitcast(i32)
        onehot64 = qbd[0:NFFT, 0:VOCAB * NBJ]
        mag = vz[0:NFREQ, 0:VOCAB * NBJ]
        dft_sb = tmp[0:NFFT, 2, 0:2 * NFREQ]
        vrow = tmp[0:NFFT, 2, 128:128 + VOCAB]
        pw_sb = tmp[0:NFREQ, 3, 0:VOCAB * D_ENC]
        pbias = tmp[0:1, 4, 0:D_ENC]
        encA = tmp[:, 4, 128:128 + D_ENC]
        encB = tmp[0:NBJ - P, 4, 256:256 + D_ENC]
        SC = 384
        NSC = VOCAB * NBJ // SC
        sq = tmp[0:NFREQ, 0:2, 0:SC]

        enc_dram = nc.dram_tensor("enc_scratch", (NBJ, D_ENC), f32, kind="Internal").ap()
        mask_dram = nc.dram_tensor("mask_scratch", (STEPS, K * E, SEQ), f16, kind="Internal").ap()

        s_wload = sem("s_wload")
        s_wo_load = sem("s_wo_load")
        s_const = sem("s_const")
        s_stft_in = sem("s_stft_in")
        s_zero = sem("s_zero")
        s_whi = sem("s_whi")
        s_wlo = sem("s_wlo")
        s_prep = sem("s_prep")
        s_oh64 = sem("s_oh64")
        s_dft = sem("s_dft")
        s_sq = sem("s_sq")
        s_msq = sem("s_msq")
        s_mag = sem("s_mag")
        s_enc = sem("s_enc")
        s_enc_sb = sem("s_enc_sb")
        s_enc_out = sem("s_enc_out")
        s_czero = sem("s_czero")
        s_mask_in = [sem("s_mask_in0"), sem("s_mask_in1")]
        s_xm = sem("s_xm")
        s_gate = sem("s_gate")
        s_tanh = sem("s_tanh")
        s_u = sem("s_u")
        s_v = sem("s_v")
        s_c = sem("s_c")
        s_tc = sem("s_tc")
        s_h = sem("s_h")
        s_hhi = sem("s_hhi")
        s_hlo = sem("s_hlo")
        s_y = sem("s_y")
        s_yadd = sem("s_yadd")
        s_out = sem("s_out")
        names = """ids enc onehot emb hsb bnst bnag veps rstd xn xnTp xnT qp kp vp q k v qbd vwin vz
            pw sw mw dw ew rw iw ow owr ow_c pf sf mf df ef rf if_ uf S mS dS eS rS iS nS prT O of0 of1
            cf attn proj h2 bnst2 bnag2 veps2 rstd2 xn2 x2p xhi x32 xlo lgp lg m1 eq1 ix1 im1 k1 l2 m2
            eq2 ix2 im2 k2 dd ed sd w0 w1 wa wb wt mwc mwp mrow wT mout bp h2b wys"""
        S = {n: sem("f_" + n) for n in names.split()}

        def is_zero(b):
            return isinstance(b, int) and b == 0

        def is_one(b):
            return isinstance(b, int) and b == 1

        def run_steps(eng, step):
            step(0, 0, True, False)
            with eng.Fori(0, (STEPS - 2) // 2) as pair:
                step(pair * 2 + 1, 1, False, False)
                step(pair * 2 + 2, 0, False, False)
            step(STEPS - 1, (STEPS - 1) % 2, False, True)

        def row(ap):
            return ap.rearrange("(a n) -> a n", a=1)

        consts = [
            (wqkv_sb[:, :], w_qkv), (bqkv_sb[:, :], b_qkv), (wout_sb[:, :], w_out),
            (rw_sb[:, :], router_w), (rb_sb[:, :], row(router_b).to_broadcast([P, E])), (bo_sb[:, :], bo),
            (bout_sb[:, :], row(b_out)), (ident[:, :], ident_dram), (hones[:, :], head_ones), (band_sb[:, :], band),
            (par_sb[:, :], parity), (m8_sb[:, :], expert_m8), (vcol[:, :], vocab_col),
            (bias_sb[:, :, :], b_lstm),
            (rows[0:ENC0 + NFR, :], frame_rows), (table[0:ENC0 + NFR, :], emb_table),
        ]

        block = ctx.enter_context(nc.Block())

        @block.sync
        def _(sp):
            def load(dst, src, s):
                sp.dma_start(dst, src).then_inc(s, 16)

            load(fid, frame_ids, s_stft_in)
            load(dft_sb, dft.rearrange("n c f -> n (c f)"), s_stft_in)
            load(vrow, vocab_rows, s_stft_in)
            load(pw_sb.rearrange("f (v o) -> f v o", v=VOCAB), proj_w.rearrange("(f v) o -> f v o", v=VOCAB), s_stft_in)
            load(pbias, proj_b.rearrange("(a n) -> a n", a=1), s_stft_in)
            for dst, src in consts:
                load(dst, src, s_const)
            load(wi_st.rearrange("p a (b n) -> p (a b) n", b=2), wi.rearrange("e i n -> i e n"), s_wload)
            load(wh_st.rearrange("p a (b n) -> p (a b) n", b=2), wh.rearrange("e i n -> i e n"), s_wload)
            load(wo_st.rearrange("p (e n) -> p e n", e=E), wo.rearrange("e i n -> i e n"), s_wo_load)
            sp.wait_ge(s_enc_sb, 2)
            load(enc_dram[0:P, :], encA, s_enc_out)
            load(enc_dram[P:NBJ, :], encB, s_enc_out)
            sp.wait_ge(s_enc_out, 32)

            def front(t, b):
                if t == 0:
                    sp_ids(b)
                if t == 5:
                    sp.wait_ge(S["q"], b + 1)
                    if not is_zero(b):
                        sp.wait_ge(S["S"], b)
                    for h in range(HEADS):
                        load(qbd[DH * h:DH * h + DH, h * TF:(h + 1) * TF], qperm[DH * h:DH * h + DH, :], S["qbd"])
                if t == 6:
                    sp.wait_ge(S["vwin"], b + 1)
                    if not is_zero(b):
                        sp.wait_ge(S["O"], b)
                    for g in range(4):
                        load(vz[32 * g:32 * g + 32, g * KB * NBLK:(g + 1) * KB * NBLK], vwin[32 * g:32 * g + 32, :], S["vz"])
                if t == 21:
                    sp.wait_ge(S["mrow"], b + 1)
                    sp.wait_ge(s_enc_out, 32)
                    load(mask_dram[bass.ds(b, 1), :, :].rearrange("a r t -> (a r) t"), mrow[:, :], S["mout"])

            def sp_ids(b):
                if not is_zero(b):
                    sp.wait_ge(S["onehot"], b)
                    sp.wait_ge(S["emb"], b)
                sp.wait_ge(s_enc_out, 32)
                load(ids[:, :], x_ids[bass.ds(b, 1), :].to_broadcast([VOCAB, SEQ]), S["ids"])
                load(table[ENC0:ENC0 + NFR, D_EMB:D],
                     enc_dram.rearrange("(b j) o -> b j o", j=NFR)[bass.ds(b, 1), :, :].rearrange("a j o -> (a j) o"),
                     S["enc"])

            def mask_in(s, e):
                if e == 0:
                    sp.wait_ge(S["mout"], (s + 1) * 16)
                if e >= 2 or not is_zero(s):
                    sp.wait_ge(s_xm, s * E + e - 1)
                sp.wait_ge(s_enc_out, 32)
                src = mask_dram[bass.ds(s, 1), :, :].rearrange("a (k e) t -> (a k) e t", k=K)[:, e, :]
                sp.dma_start(masks[:, e % 2, :, :], src.rearrange("(a k) t -> a k t", a=1)
                             .to_broadcast([P, K, SEQ])).then_inc(s_mask_in[e % 2], 16)

            def store(s, par):
                sp.wait_ge(s_yadd, (s + 1) * (K * E))
                sp.wait_ge(s_enc_out, 32)
                sp.dma_start(out[bass.ds(s, 1), :, :].rearrange("a (t p) d -> p (a t) d", p=P),
                             h2[:, par, :, :]).then_inc(s_out, 16)

            def step(s, par, first, last):
                for t in range(NG * E):
                    e, g = t // NG, t % NG
                    if t == 8 and not first:
                        store(s - 1, 1 - par)
                    if not last:
                        front(t, s + 1)
                    if g == 2 and e < E - 2:
                        mask_in(s, e + 2)
                    if g == 2 and e >= E - 2 and not last:
                        mask_in(s + 1, e + 2 - E)

            for t in range(NG * E):
                front(t, 0)
            mask_in(0, 0)
            mask_in(0, 1)
            run_steps(sp, step)
            store(STEPS - 1, (STEPS - 1) % 2)
            sp.wait_ge(s_out, 16 * STEPS)

        @block.tensor
        def _(pe):
            mm = nc.tensor.matmul

            pe.wait_ge(s_stft_in, 80)
            pe.wait_ge(s_oh64, 1)
            for c in range(NSC):
                if c >= 2:
                    pe.wait_ge(s_sq, 2 * (c - 1))
                for r in range(2):
                    mm(gates[0:NFREQ, c % 2, r * SEQ:r * SEQ + SC], dft_sb[:, r * NFREQ:(r + 1) * NFREQ],
                       onehot64[:, c * SC:(c + 1) * SC], start=True, stop=True).then_inc(s_dft, 1)
            pe.wait_ge(s_mag, 1)
            pe.wait_ge(s_prep, 1)
            for r, (c0, n) in enumerate(((0, P), (P, NBJ - P))):
                dst = (FA[0:n, r, 0:D_ENC])
                for v in range(VOCAB):
                    mm(dst, mag[:, v * NBJ + c0:v * NBJ + c0 + n], pw_sb[:, v * D_ENC:(v + 1) * D_ENC],
                       start=(v == 0), stop=False)
                mm(dst, ones1[0:1, 0:n], pbias, start=False, stop=True).then_inc(s_enc, 1)

            def front(t, b):
                b1 = b + 1
                if t == 1:
                    pe.wait_ge(S["onehot"], b1)
                    pe.wait_ge(S["enc"], 16 * b1)
                    for i in range(TILES):
                        last = mm(FB[:, i * D:(i + 1) * D], rows[:, i * P:(i + 1) * P], table[:, :],
                                  start=True, stop=True)
                    last.then_inc(S["emb"], 1)
                if t == 3:
                    pe.wait_ge(S["xn"], b1)
                    pe.wait_ge(S["hsb"], b1)
                    for i in range(TILES):
                        last = nc.tensor.transpose(FB[:, i * P:(i + 1) * P], xn[:, i, :], ident[:, :])
                    last.then_inc(S["xnTp"], 1)
                if t == 4:
                    pe.wait_ge(S["xnT"], b1)
                    for j, dst, s in ((0, FA[:, 0, :], "qp"), (1, FA[:, 1, :], "kp"), (2, FB[:, :], "vp")):
                        mm(dst, wqkv_sb[:, j * D:(j + 1) * D], xnT[:, :], start=True, stop=True).then_inc(S[s], 1)
                if t == 6:
                    pe.wait_ge(S["pw"], b1)
                    pe.wait_ge(S["v"], b1)
                    mm(FB[:, :], hones[:, :], prod[:, :], start=True, stop=True).then_inc(S["sw"], 1)
                if t == 7:
                    pe.wait_ge(S["qbd"], 128 * b1)
                    pe.wait_ge(S["q"], b1)
                    pe.wait_ge(S["k"], b1)
                    for r in range(2):
                        mm(FA[:, r, 0:HB * KB], identb[:, :],
                           bandb[:, :].rearrange("p (a k) -> p a k", a=1).to_broadcast([P, HB, KB]),
                           start=True, stop=False, skip_group_check=True)
                        for jj in range(HB):
                            j = r * HB + jj
                            last = mm(FA[:, r, jj * KB:(jj + 1) * KB], qbd[:, j::NBLK],
                                      kf[:, j * QB:j * QB + KB], start=False, stop=(jj == HB - 1),
                                      skip_group_check=True)
                    last.then_inc(S["S"], 1)
                if t == 8:
                    pe.wait_ge(S["pf"], b1)
                    mm(FB[:, 0:TF], hones[:, :], prod[:, 0:TF], start=True, stop=True).then_inc(S["sf"], 1)
                if t == 11:
                    pe.wait_ge(S["prT"], b1)
                    pe.wait_ge(S["vz"], 64 * b1)
                    for j in range(NBLK):
                        last = mm(FA[:, j // HB, (j % HB) * KB:(j % HB + 1) * KB], vz[:, j::NBLK],
                                  prT[:, j * KB:(j + 1) * KB], start=True, stop=True)
                    last.then_inc(S["O"], 1)
                if t == 13:
                    pe.wait_ge(S["attn"], b1)
                    for i in range(TILES):
                        mm(FB[:, i * D:(i + 1) * D], attn[:, i * P:(i + 1) * P], wout_sb[:, :], start=True, stop=False)
                        last = mm(FB[:, i * D:(i + 1) * D], ones1[:, :], bout_sb[:, :], start=False, stop=True)
                    last.then_inc(S["proj"], 1)
                if t == 15:
                    pe.wait_ge(S["xn2"], b1)
                    for i in range(TILES):
                        last = nc.tensor.transpose(FB[:, i * P:(i + 1) * P], xn[:, i, :], ident[:, :])
                    last.then_inc(S["x2p"], 1)
                if t == 17:
                    pe.wait_ge(S["x32"], b1)
                    pe.wait_ge(S["xlo"], b1)
                    for i in range(TILES):
                        last = mm(FB[:, i * E:(i + 1) * E], x32[:, i * P:(i + 1) * P], rw_sb[:, :], start=True, stop=True)
                    last.then_inc(S["lgp"], 1)
                if t == 21:
                    pe.wait_ge(S["mwc"], b1)
                    for i in range(TILES):
                        nc.tensor.transpose(FB[0:K * E, i * P:(i + 1) * P], mk[:, i, :], ident[:, :])
                    for i in range(TILES):
                        last = nc.tensor.transpose(FA[0:E, 1, i * P:(i + 1) * P], mw[:, i, :], ident[:, :])
                    last.then_inc(S["mwp"], 1)
                if t == 22:
                    pe.wait_ge(S["wT"], b1)
                    for i in range(TILES):
                        last = mm(FA[:, 0, i * D:(i + 1) * D], wT[:, i * P:(i + 1) * P], bo_sb[:, :], start=True, stop=True)
                    last.then_inc(S["bp"], 1)

            def unit_gate(s, e, g, first):
                gate = ORDER[g]
                slot = g % 2
                if not (first and e == 0 and g < 2):
                    pe.wait_ge(s_tanh, s * (E * NG) + e * NG + g - 1)
                if g == 0:
                    pe.wait_ge(s_xm, s * E + e + 1)
                    if not first:
                        pe.wait_ge(s_hlo, s * E + e - E + 1)
                parts = [(wi_sb, lambda k, v: xm[:, e % 2, k, v, :])]
                if not first:
                    parts.append((wh_sb, lambda k, v: Hs[:, e, v, k * SEQ:(k + 1) * SEQ]))
                seq = []
                for w, mov in parts:
                    for wpart, vpart in ((HI, HI), (HI, LO), (LO, HI)):
                        for k in range(K):
                            seq.append((w[:, e, wpart, gate * P:(gate + 1) * P], mov(k, vpart), k))
                for n, (w, v, k) in enumerate(seq):
                    last = mm(gates[:, slot, k * SEQ:(k + 1) * SEQ], w, v, start=(n < K), stop=(n >= len(seq) - K))
                last.then_inc(s_gate, 1)

            def unit_y(s, e, k, yfirst):
                pe.wait_ge(s_hlo, s * E + e + 1)
                if not yfirst:
                    pe.wait_ge(s_yadd, s * (E * K) + e * K + k)
                for i in range(TILES):
                    tok = slice(k * SEQ + i * P, k * SEQ + (i + 1) * P)
                    mm(yp[:, i, :], Hs[:, e, HI, tok], wo_sb[:, e, HI, :], start=True, stop=False)
                    mm(yp[:, i, :], Hs[:, e, HI, tok], wo_sb[:, e, LO, :], start=False, stop=False)
                    last = mm(yp[:, i, :], Hs[:, e, LO, tok], wo_sb[:, e, HI, :], start=False, stop=True)
                last.then_inc(s_y, 1)

            def step(s, par, first, last):
                for t in range(NG * E):
                    e, g = t // NG, t % NG
                    unit_gate(s, e, g, first)
                    if g in (0, 2):
                        if e >= 2:
                            unit_y(s, e - 2, g // 2, first and e == 2 and g == 0)
                        elif not first:
                            unit_y(s - 1, e - 2 + E, g // 2, False)
                    if not last:
                        front(t, s + 1)

            pe.wait_ge(s_const, 16 * len(consts))
            pe.wait_ge(s_zero, 1)
            pe.wait_ge(s_prep, 4)
            for t in range(NG * E):
                front(t, 0)
            pe.wait_ge(s_wlo, 9)
            run_steps(pe, step)
            for e in (E - 2, E - 1):
                for k in range(K):
                    unit_y(STEPS - 1, e, k, False)

        @block.scalar
        def _(act):
            A = nc.scalar.activation
            for c in range(NSC):
                act.wait_ge(s_dft, 2 * c + 2)
                if c >= 1:
                    act.wait_ge(s_msq, c)
                for r in range(2):
                    A(sq[:, r, :], gates[0:NFREQ, c % 2, r * SEQ:r * SEQ + SC], ACT.Square).then_inc(s_sq, 1)
            act.wait_ge(s_msq, NSC)
            A(mag, mag, ACT.Sqrt).then_inc(s_mag, 1)
            act.wait_ge(s_enc, 2)
            A(encA, FA[:, 0, 0:D_ENC], ACT.Copy).then_inc(s_enc_sb, 1)
            A(encB, FA[0:NBJ - P, 1, 0:D_ENC], ACT.Copy).then_inc(s_enc_sb, 1)
            act.wait_ge(s_const, 16 * len(consts))

            def front(t, b):
                b1 = b + 1
                if t == 1:
                    act.wait_ge(S["emb"], b1)
                    if not is_zero(b):
                        act.wait_ge(S["h2"], b)
                    A(h_sb[:, :, :].rearrange("p t d -> p (t d)"), FB[:, :], ACT.Copy).then_inc(S["hsb"], 1)
                if t == 3:
                    act.wait_ge(S["xnTp"], b1)
                    A(xnT[:, :], FB[:, :], ACT.Copy).then_inc(S["xnT"], 1)
                if t == 4:
                    act.wait_ge(s_prep, 4)
                    act.wait_ge(S["qp"], b1)
                    if not is_zero(b):
                        act.wait_ge(S["qbd"], 128 * b)
                    A(qT[:, :], FA[:, 0, :], ACT.Identity, bias=bqkv_sb[:, 0:1], scale=DH ** -0.5)
                    if not is_zero(b):
                        act.wait_ge(S["bp"], b)
                    A(qperm.rearrange("p (q j) -> p j q", j=NBLK), FA[:, 0, NW:SEQ].rearrange("p (j q) -> p j q", j=NBLK),
                      ACT.Identity, bias=bqkv_sb[:, 0:1], scale=DH ** -0.5).then_inc(S["q"], 1)
                    act.wait_ge(S["kp"], b1)
                    A(kw[:, :], FA[:, 1, 0:NW], ACT.Identity, bias=bqkv_sb[:, 1:2])
                    A(kf[:, PAD:PAD + TF], FA[:, 1, NW:SEQ], ACT.Identity, bias=bqkv_sb[:, 1:2]).then_inc(S["k"], 1)
                    act.wait_ge(S["vp"], b1)
                    A(vw[:, :], FB[:, 0:NW], ACT.Identity, bias=bqkv_sb[:, 2:3])
                    A(vf[:, PAD:PAD + TF], FB[:, NW:SEQ], ACT.Identity, bias=bqkv_sb[:, 2:3]).then_inc(S["v"], 1)
                if t == 6:
                    act.wait_ge(S["dw"], b1)
                    if not is_zero(b):
                        act.wait_ge(S["mout"], 16 * b)
                    A(ew[:, :], prod[:, :], ACT.Exp).then_inc(S["ew"], 1)
                if t == 8:
                    act.wait_ge(S["dS"], b1)
                    A(pr[:, :], pr[:, :], ACT.Exp).then_inc(S["eS"], 1)
                if t == 9:
                    act.wait_ge(S["df"], b1)
                    A(ew[:, 0:TF], prod[:, 0:TF], ACT.Exp).then_inc(S["ef"], 1)
                if t == 15:
                    act.wait_ge(S["x2p"], b1)
                    A(xs[:, par_of(b), HI, :], FB[:, :], ACT.Copy, scale=V_SCALE).then_inc(S["xhi"], 1)
                    A(x32[:, :], FB[:, :], ACT.Copy).then_inc(S["x32"], 1)
                if t == 19:
                    act.wait_ge(S["dd"], b1)
                    A(m4[:, 6, :], m4[:, 5, :], ACT.Exp).then_inc(S["ed"], 1)
                if t == 21:
                    act.wait_ge(S["mwp"], b1)
                    if not is_zero(b):
                        act.wait_ge(S["mout"], 16 * b)
                    A(mrow[:, :], FB[0:K * E, :], ACT.Copy).then_inc(S["mrow"], 1)

            def gate_tanh(s, e, g, first):
                gate = ORDER[g]
                act.wait_ge(s_gate, s * (E * NG) + e * NG + g + 1)
                if not (first and e == 0):
                    if gate == O:
                        act.wait_ge(s_hlo, s * E + e)
                    else:
                        act.wait_ge(s_c, s * E + e)
                A(tmp[:, gate, :], gates[:, g % 2, :], ACT.Tanh, bias=bias_sb[:, e, gate:gate + 1],
                  scale=UNSCALE).then_inc(s_tanh, 1)

            def cell_tanh(s, e):
                act.wait_ge(s_c, s * E + e + 1)
                A(tmp[:, 4, :], C[:, e, :], ACT.Tanh, scale=0.5).then_inc(s_tc, 1)

            def split_hi(s, e):
                act.wait_ge(s_h, s * E + e + 1)
                A(Hs[:, e, HI, :], tmp[:, O, :], ACT.Copy, scale=V_SCALE).then_inc(s_hhi, 1)

            def step(s, par, first, last):
                for t in range(NG * E):
                    e, g = t // NG, t % NG
                    if g == 0 and e:
                        split_hi(s, e - 1)
                    elif g == 0 and not first:
                        split_hi(s - 1, E - 1)
                    gate_tanh(s, e, g, first)
                    if ORDER[g] == F:
                        cell_tanh(s, e)
                    if not last:
                        front(t, s + 1)

            par_of = lambda b: PAR[0]
            PAR = [0]

            def split_w_hi():
                for src, dst, f, s_n in ((wi_st, wi_sb, 1.0, 16), (wh_st, wh_sb, 0.5, 32)):
                    act.wait_ge(s_wload, 32)
                    v = src.rearrange("p a (b n) -> p (a b) n", b=2)
                    for c0, c1, half in ((0, 2, 0.5), (2, 3, 1.0), (3, 4, 0.5)):
                        A(dst[:, :, HI, c0 * P:c1 * P], v[:, :, c0 * P:c1 * P], ACT.Copy,
                          scale=W_SCALE * f * half).then_inc(s_whi, 1)
                act.wait_ge(s_wo_load, 16)
                A(wo_sb[:, :, HI, :], wo_st.rearrange("p (e n) -> p e n", e=E), ACT.Copy,
                  scale=W_SCALE * 0.5).then_inc(s_whi, 1)

            split_w_hi()
            for t in range(NG * E):
                front(t, 0)

            def step_p(s, par, first, last):
                PAR[0] = 1 - par
                step(s, par, first, last)

            run_steps(act, step_p)
            split_hi(STEPS - 1, E - 1)

        @block.vector
        def _(dve):
            V = nc.vector
            TT, TS, STT = V.tensor_tensor, V.tensor_scalar, V.scalar_tensor_tensor
            dve.wait_ge(s_stft_in, 80)
            TT(onehot64.rearrange("p (v n) -> p v n", v=VOCAB),
               fid.rearrange("p (a n) -> p a n", a=1).to_broadcast([NFFT, VOCAB, NBJ]),
               vrow.rearrange("p (v a) -> p v a", a=1).to_broadcast([NFFT, VOCAB, NBJ]), ALU.is_equal).then_inc(s_oh64, 1)
            V.memset(ones1[:, :], 1.0).then_inc(s_prep, 1)
            dve.wait_ge(s_const, 16 * len(consts))
            V.tensor_copy(identb[:, :], ident[:, :]).then_inc(s_prep, 1)
            V.tensor_copy(bandb[:, :], band_sb[:, :]).then_inc(s_prep, 1)
            TS(bqkv_sb[:, 0:1], bqkv_sb[:, 0:1], DH ** -0.5, None, ALU.mult)
            TS(bias_sb[:, :, I:F + 1], bias_sb[:, :, I:F + 1], 0.5, None, ALU.mult)
            TS(bias_sb[:, :, O:O + 1], bias_sb[:, :, O:O + 1], 0.5, None, ALU.mult).then_inc(s_prep, 1)
            for c in range(NSC):
                dve.wait_ge(s_sq, 2 * c + 2)
                TT(mag[:, c * SC:(c + 1) * SC], sq[:, 0, :], sq[:, 1, :], ALU.add).then_inc(s_msq, 1)
            n = 0
            for src, dst, f in ((wi_st, wi_sb, 1.0), (wh_st, wh_sb, 0.5)):
                v = src.rearrange("p a (b n) -> p (a b) n", b=2)
                for c0, c1, half in ((0, 2, 0.5), (2, 3, 1.0), (3, 4, 0.5)):
                    n += 1
                    dve.wait_ge(s_whi, n)
                    STT(out=dst[:, :, LO, c0 * P:c1 * P], in0=v[:, :, c0 * P:c1 * P], scalar=W_SCALE * f * half,
                        in1=dst[:, :, HI, c0 * P:c1 * P], op0=ALU.mult, op1=ALU.subtract).then_inc(s_wlo, 1)
            dve.wait_ge(s_whi, 7)
            STT(out=wo_sb[:, :, LO, :], in0=wo_st.rearrange("p (e n) -> p e n", e=E), scalar=W_SCALE * 0.5,
                in1=wo_sb[:, :, HI, :], op0=ALU.mult, op1=ALU.subtract).then_inc(s_wlo, 1)
            dve.wait_ge(s_wlo, 7)
            V.memset(C[:, :, :].rearrange("p e n -> p (e n)"), 0.0).then_inc(s_wlo, 1)
            V.memset(Hs[:, 0, 0, 0:2], 0.0).then_inc(s_wlo, 1)

            def wait(name, n):
                dve.wait_ge(S[name], n)

            def norm_stats(src, names):
                for i in range(TILES):
                    last = V.bn_stats(stats[:, i, :], src(i))
                last.then_inc(S[names[0]], 1)
                return last

            def c3(ap, n):
                return ap.rearrange("p (n c) -> p n c", n=n)

            def bc(ap, n, c):
                return ap.rearrange("p (n a) -> p n a", a=1).to_broadcast([P, n, c])

            def front(t, b, q):
                b1 = b + 1
                if t == 0:
                    wait("ids", 16 * b1)
                    if not is_zero(b):
                        wait("emb", b)
                    TS(rows[0:VOCAB, :], ids[:, :], vcol[:, 0:1], None, ALU.is_equal).then_inc(S["onehot"], 1)
                if t == 1:
                    wait("hsb", b1)
                    norm_stats(lambda i: h_sb[:, i, :], ("bnst",))
                    wait("bnst", b1)
                    V.memset(spare[:, :], 0.0)
                    for i in range(TILES):
                        last = V.bn_aggr(mv[:, i, :], stats[:, i, :])
                    last.then_inc(S["bnag"], 1)
                    wait("bnag", b1)
                    TS(veps[:, :], mv[:, :, 1], EPS, None, ALU.add).then_inc(S["veps"], 1)
                if t == 2:
                    wait("rstd", b1)
                    wait("hsb", b1)
                    for i in range(TILES):
                        last = TS(xn[:, i, :], h_sb[:, i, :], mv[:, i, 0:1], rstd[:, i:i + 1], ALU.subtract, ALU.mult)
                    last.then_inc(S["xn"], 1)
                if t == 5:
                    wait("q", b1)
                    wait("k", b1)
                    wait("v", b1)
                    p3 = c3(prod[:, :], NW)
                    TT(p3[:, :, 0], qT[:, 0:NW], kw[:, :], ALU.mult)
                    TT(p3[:, :, 1:CH + 1], bc(qT[:, 0:NW], NW, CH), c3(kf[:, PAD:PAD + TF], NW), ALU.mult).then_inc(S["pw"], 1)
                    if not is_zero(b):
                        wait("O", b)
                    src = vf[:, :]
                    win = bass.AP(tensor=src.tensor, offset=src.offset, ap=[list(src.ap[0]), [QB, NBLK], [1, KB]])
                    V.transpose(vwin[:, :].rearrange("p (c j) -> p j c", j=NBLK), win).then_inc(S["vwin"], 1)
                if t == 6:
                    wait("sw", b1)
                    s3 = c3(FB[:, :], NW)
                    V.tensor_reduce(red[:, :], s3, axis=X, op=ALU.max).then_inc(S["mw"], 1)
                    wait("mw", b1)
                    TT(c3(prod[:, :], NW), s3, bc(red[:, :], NW, CH + 1), ALU.subtract).then_inc(S["dw"], 1)
                if t == 7:
                    wait("ew", b1)
                    e3 = c3(ew[:, :], NW)
                    V.tensor_reduce(red[:, :], e3, axis=X, op=ALU.add).then_inc(S["rw"], 1)
                    wait("rw", b1)
                    V.reciprocal(red2[:, :], red[:, :]).then_inc(S["iw"], 1)
                    p3 = c3(prod[:, :], NW)
                    TT(p3[:, :, 0], e3[:, :, 0], vw[:, :], ALU.mult)
                    TT(p3[:, :, 1:CH + 1], e3[:, :, 1:CH + 1], c3(vf[:, PAD:PAD + TF], NW), ALU.mult).then_inc(S["ow"], 1)
                    wait("ow", b1)
                    V.tensor_reduce(red3[:, :], p3, axis=X, op=ALU.add).then_inc(S["owr"], 1)
                    wait("owr", b1)
                    wait("iw", b1)
                    TT(oW[:, :], red3[:, :], red2[:, :], ALU.mult).then_inc(S["ow_c"], 1)
                    wait("ow_c", b1)
                    TT(c3(prod[:, 0:TF], NW), c3(qT[:, NW:SEQ], NW), bc(oW[:, :], NW, CH), ALU.mult).then_inc(S["pf"], 1)
                if t == 8:
                    wait("S", b1)
                    s4 = FA[:, :, 0:HB * KB].rearrange("p r (j k) -> p r j k", k=KB)
                    V.tensor_reduce(wred[:, 0, :].rearrange("p (r j) -> p r j", r=2), s4, axis=X, op=ALU.max).then_inc(S["mS"], 1)
                    wait("mS", b1)
                    TT(pr[:, :].rearrange("p (r j k) -> p r j k", r=2, k=KB), s4,
                       wred[:, 0, :].rearrange("p (r j a) -> p r j a", r=2, a=1).to_broadcast([P, 2, HB, KB]),
                       ALU.subtract).then_inc(S["dS"], 1)
                if t == 9:
                    wait("sf", b1)
                    s3 = c3(FB[:, 0:TF], NW)
                    V.tensor_reduce(red[:, :], s3, axis=X, op=ALU.max).then_inc(S["mf"], 1)
                    wait("mf", b1)
                    TT(c3(prod[:, 0:TF], NW), s3, bc(red[:, :], NW, CH), ALU.subtract).then_inc(S["df"], 1)
                if t == 10:
                    wait("eS", b1)
                    V.tensor_reduce(wred[:, 1, :], c3(pr[:, :], NBLK), axis=X, op=ALU.add).then_inc(S["rS"], 1)
                    wait("rS", b1)
                    V.reciprocal(wred[:, 2, :], wred[:, 1, :]).then_inc(S["iS"], 1)
                    wait("iS", b1)
                    TT(c3(pr[:, :], NBLK), c3(pr[:, :], NBLK), bc(wred[:, 2, :], NBLK, KB), ALU.mult).then_inc(S["nS"], 1)
                    wait("nS", b1)
                    wait("vz", 64 * b1)
                    V.transpose(prT[:, :], pr[:, :]).then_inc(S["prT"], 1)
                if t == 11:
                    wait("ef", b1)
                    e3 = c3(ew[:, 0:TF], NW)
                    V.tensor_reduce(red[:, :], e3, axis=X, op=ALU.add).then_inc(S["rf"], 1)
                    wait("rf", b1)
                    V.reciprocal(red2[:, :], red[:, :]).then_inc(S["if_"], 1)
                    wait("if_", b1)
                    TT(red3[:, :], oW[:, :], red2[:, :], ALU.mult).then_inc(S["uf"], 1)
                    wait("uf", b1)
                    V.tensor_copy(attn[:, 0:NW], oW[:, :])
                    TT(c3(attn[:, NW:SEQ], NW), e3, bc(red3[:, :], NW, CH), ALU.mult).then_inc(S["cf"], 1)
                    wait("cf", b1)
                if t == 12:
                    wait("O", b1)
                    for par2 in range(2):
                        for r in range(2):
                            o3 = FA[:, r, 0:HB * KB].rearrange("p (j c q) -> p j c q", c=2, q=QB)[:, :, par2, :]
                            a3 = attn[:, NW + r * HB * QB:NW + (r + 1) * HB * QB].rearrange("p (j q) -> p j q", q=QB)
                            last = STT(out=a3, in0=o3, scalar=par_sb[:, par2:par2 + 1], in1=a3, op0=ALU.mult, op1=ALU.add)
                        if par2 == 0:
                            last.then_inc(S["of0"], 1)
                            wait("of0", b1)
                    last.then_inc(S["attn"], 1)
                if t == 13:
                    wait("proj", b1)
                    if not (is_zero(b) or is_one(b)):
                        dve.wait_ge(s_out, 16 * (b - 1))
                    TT(h2[:, q, :, :].rearrange("p t d -> p (t d)"), FB[:, :],
                       h_sb[:, :, :].rearrange("p t d -> p (t d)"), ALU.add).then_inc(S["h2"], 1)
                    wait("h2", b1)
                    norm_stats(lambda i: h2[:, q, i, :], ("bnst2",))
                    wait("bnst2", b1)
                    V.memset(spare[:, :], 0.0)
                    for i in range(TILES):
                        last = V.bn_aggr(mv[:, i, :], stats[:, i, :])
                    last.then_inc(S["bnag2"], 1)
                    wait("bnag2", b1)
                    TS(veps[:, :], mv[:, :, 1], EPS, None, ALU.add).then_inc(S["veps2"], 1)
                if t == 14:
                    wait("rstd2", b1)
                    for i in range(TILES):
                        last = TS(xn[:, i, :], h2[:, q, i, :], mv[:, i, 0:1], rstd[:, i:i + 1], ALU.subtract, ALU.mult)
                    last.then_inc(S["xn2"], 1)
                if t == 16:
                    wait("x32", b1)
                    STT(out=xs[:, q, LO, :], in0=FB[:, :], scalar=V_SCALE, in1=xs[:, q, HI, :],
                        op0=ALU.mult, op1=ALU.subtract).then_inc(S["xlo"], 1)
                L, EQ, IX, K1, L2, EQ2, IX2, K2 = (lg[:, i, :, :] for i in range(8))
                M = lambda i: m4[:, i, :]
                Mb = lambda i: m4[:, i, :].rearrange("p (t a) -> p t a", a=1).to_broadcast([P, TILES, E])
                e8 = m8_sb[:, :].rearrange("p (a e) -> p a e", a=1).to_broadcast([P, TILES, E])
                if t == 17:
                    wait("lgp", b1)
                    TT(L, FB[:, 0:TILES * E].rearrange("p (t e) -> p t e", e=E),
                       rb_sb[:, :].rearrange("p (a e) -> p a e", a=1).to_broadcast([P, TILES, E]), ALU.add).then_inc(S["lg"], 1)
                    wait("lg", b1)
                    V.tensor_reduce(M(0), L, axis=X, op=ALU.max).then_inc(S["m1"], 1)
                    wait("m1", b1)
                    TT(EQ, L, Mb(0), ALU.is_ge).then_inc(S["eq1"], 1)
                    wait("eq1", b1)
                    TT(IX, EQ, e8, ALU.mult).then_inc(S["ix1"], 1)
                    wait("ix1", b1)
                    V.tensor_reduce(M(1), IX, axis=X, op=ALU.min).then_inc(S["im1"], 1)
                if t == 18:
                    wait("im1", b1)
                    TT(K1, e8, Mb(1), ALU.is_equal).then_inc(S["k1"], 1)
                    wait("k1", b1)
                    STT(out=L2, in0=K1, scalar=-3.0e38, in1=L, op0=ALU.mult, op1=ALU.add).then_inc(S["l2"], 1)
                    wait("l2", b1)
                    V.tensor_reduce(M(2), L2, axis=X, op=ALU.max).then_inc(S["m2"], 1)
                    wait("m2", b1)
                    TT(M(5), M(2), M(0), ALU.subtract).then_inc(S["dd"], 1)
                    TT(EQ2, L2, Mb(2), ALU.is_ge).then_inc(S["eq2"], 1)
                    wait("eq2", b1)
                    TT(IX2, EQ2, e8, ALU.mult).then_inc(S["ix2"], 1)
                    wait("ix2", b1)
                    V.tensor_reduce(M(3), IX2, axis=X, op=ALU.min).then_inc(S["im2"], 1)
                    wait("im2", b1)
                    TT(K2, e8, Mb(3), ALU.is_equal).then_inc(S["k2"], 1)
                if t == 20:
                    wait("ed", b1)
                    TS(M(7), M(6), 1.0, None, ALU.add).then_inc(S["sd"], 1)
                    wait("sd", b1)
                    V.reciprocal(M(8), M(7)).then_inc(S["w0"], 1)
                    wait("w0", b1)
                    TT(M(9), M(8), M(6), ALU.mult).then_inc(S["w1"], 1)
                    wait("w1", b1)
                    wait("k2", b1)
                    TT(IX, K1, Mb(8), ALU.mult).then_inc(S["wa"], 1)
                    TT(IX2, K2, Mb(9), ALU.mult).then_inc(S["wb"], 1)
                    V.tensor_copy(mk[:, :, 0:E], K1)
                    V.tensor_copy(mk[:, :, E:2 * E], K2)
                    wait("wb", b1)
                    TT(mw[:, :, :], IX, IX2, ALU.add).then_inc(S["mwc"], 1)
                    TS(wy[:, q, :, 0, :], IX, UNSCALE, None, ALU.mult)
                    TS(wy[:, q, :, 1, :], IX2, UNSCALE, None, ALU.mult).then_inc(S["wys"], 1)
                if t == 21:
                    wait("mwp", b1)
                    V.tensor_copy(wT[:, :], FA[0:E, 1, :]).then_inc(S["wT"], 1)
                if t == 23:
                    wait("bp", b1)
                    flat = h2[:, q, :, :].rearrange("p t d -> p (t d)")
                    TT(flat, flat, FA[:, 0, :], ALU.add).then_inc(S["h2b"], 1)

            def masked_input(s, e, par, xfirst):
                dve.wait_ge(s_mask_in[e % 2], s * (16 * E // 2) + 16 * (e // 2 + 1))
                if e == 0:
                    dve.wait_ge(S["xlo"], s + 1)
                if not xfirst:
                    dve.wait_ge(s_gate, s * (E * NG) + (e - 1) * NG)
                xv = xs[:, par, :, :].rearrange("p (a v) t -> p a v t", a=1).to_broadcast([P, K, 2, SEQ])
                mv_ = masks[:, e % 2, :, :].rearrange("p k (a t) -> p k a t", a=1).to_broadcast([P, K, 2, SEQ])
                TT(xm[:, e % 2, :, :, :], xv, mv_, ALU.mult).then_inc(s_xm, 1)

            def hidden(s, e):
                dve.wait_ge(s_tc, s * E + e + 1)
                dve.wait_ge(s_tanh, s * (E * NG) + e * NG + 4)
                STT(out=tmp[:, O, :], in0=tmp[:, O, :], scalar=1.0, in1=tmp[:, 4, :],
                    op0=ALU.add, op1=ALU.mult).then_inc(s_h, 1)

            def hidden_lo(s, e):
                dve.wait_ge(s_hhi, s * E + e + 1)
                STT(out=Hs[:, e, LO, :], in0=tmp[:, O, :], scalar=V_SCALE, in1=Hs[:, e, HI, :],
                    op0=ALU.mult, op1=ALU.subtract).then_inc(s_hlo, 1)

            def input_part(s, e):
                dve.wait_ge(s_tanh, s * (E * NG) + e * NG + 2)
                STT(out=tmp[:, I, :], in0=tmp[:, I, :], scalar=1.0, in1=tmp[:, G, :],
                    op0=ALU.add, op1=ALU.mult).then_inc(s_u, 1)

            def cell(s, e):
                dve.wait_ge(s_tanh, s * (E * NG) + e * NG + 3)
                STT(out=tmp[:, F, :], in0=tmp[:, F, :], scalar=1.0, in1=C[:, e, :],
                    op0=ALU.add, op1=ALU.mult).then_inc(s_v, 1)
                dve.wait_ge(s_v, s * E + e + 1)
                dve.wait_ge(s_u, s * E + e + 1)
                STT(out=C[:, e, :], in0=tmp[:, F, :], scalar=0.5, in1=tmp[:, I, :],
                    op0=ALU.mult, op1=ALU.add).then_inc(s_c, 1)

            def add_y(s, e, k, par):
                y1 = s * (E * K) + e * K + k
                dve.wait_ge(s_y, y1 + 1)
                if e == 0 and k == 0:
                    dve.wait_ge(S["h2b"], s + 1)
                else:
                    dve.wait_ge(s_yadd, y1)
                for i in range(TILES):
                    last = STT(out=h2[:, par, i, :], in0=yp[:, i, :], scalar=wy[:, par, i, k, e:e + 1],
                               in1=h2[:, par, i, :], op0=ALU.mult, op1=ALU.add)
                last.then_inc(s_yadd, 1)

            def step(s, par, first, last):
                for t in range(NG * E):
                    e, g = t // NG, t % NG
                    if g == 0:
                        if e < E - 1:
                            masked_input(s, e + 1, par, first and e == 0)
                        elif not last:
                            masked_input(s + 1, 0, 1 - par, False)
                        if e:
                            hidden_lo(s, e - 1)
                        elif not first:
                            hidden_lo(s - 1, E - 1)
                    if g in (1, 3):
                        if e >= 2:
                            add_y(s, e - 2, g // 2, par)
                        elif not first:
                            add_y(s - 1, e - 2 + E, g // 2, 1 - par)
                    if g == 1:
                        input_part(s, e)
                    if g == 2:
                        cell(s, e)
                    if g == 3:
                        hidden(s, e)
                    if not last:
                        front(t, s + 1, 1 - par)

            dve.wait_ge(s_zero, 1)
            for t in range(NG * E):
                front(t, 0, 0)
            masked_input(0, 0, 0, True)
            run_steps(dve, step)
            hidden_lo(STEPS - 1, E - 1)
            for e in (E - 2, E - 1):
                for k in range(K):
                    add_y(STEPS - 1, e, k, (STEPS - 1) % 2)

        @block.gpsimd
        def _(pool):
            G_ = nc.gpsimd
            G_.memset(kf[:, 0:PAD], 0.0)
            G_.memset(kf[:, PAD + TF:], 0.0)
            G_.memset(vf[:, 0:PAD], 0.0)
            G_.memset(vf[:, PAD + TF:], 0.0)
            G_.memset(mhalf[:, :], -0.5)
            pool.wait_ge(s_dft, 2 * NSC)
            G_.memset(qbd[:, :], 0.0)
            pool.wait_ge(s_enc, 2)
            G_.memset(vz[:, :], 0.0).then_inc(s_zero, 1)

            def front(t, b):
                b1 = b + 1
                for tt, ve, rs in ((1, "veps", "rstd"), (13, "veps2", "rstd2")):
                    if t == tt:
                        pool.wait_ge(S[ve], b1)
                        G_.tensor_tensor(rstd[:, :], veps[:, :], mhalf[:, :], ALU.pow).then_inc(S[rs], 1)

            def step(s, par, first, last):
                if not last:
                    for t in range(NG * E):
                        front(t, s + 1)

            pool.wait_ge(s_zero, 1)
            for t in range(NG * E):
                front(t, 0)
            run_steps(pool, step)


def kernel(**inputs):
    import numpy as np
    import concourse.bacc as bacc
    from concourse import mybir as mb
    from concourse.bass_utils import run_bass_kernel_spmd as run

    ids = np.ascontiguousarray(inputs["x"])
    STEPS, SEQ = ids.shape
    NFFT, VOCAB, ENC0, D_EMB, D = 64, 16, 32, 89, 128
    NFR, NFREQ, P, DH, PAD, QB, E = SEQ // NFFT + 1, NFFT // 2 + 1, 128, 16, 8, 16, 8
    pos = np.arange(NFR)[None, :] * NFFT + np.arange(NFFT)[:, None] - NFFT // 2
    pos = np.abs(pos)
    pos = np.where(pos > SEQ - 1, 2 * (SEQ - 1) - pos, pos)
    frames = np.ascontiguousarray(ids[:, pos].transpose(1, 0, 2).reshape(NFFT, STEPS * NFR))
    n = np.arange(NFFT)
    window = 0.5 - 0.5 * np.cos(2.0 * np.pi * n / NFFT)
    ang = 2.0 * np.pi * np.outer(n, np.arange(NFREQ)) / NFFT
    dft = np.stack([window[:, None] * np.cos(ang), window[:, None] * np.sin(ang)], axis=1).astype(np.float32)
    frame_rows = np.zeros((ENC0 + NFR, SEQ), np.float32)
    frame_rows[ENC0 + np.arange(SEQ) * NFR // SEQ, np.arange(SEQ)] = 1.0
    table = np.zeros((ENC0 + NFR, D), np.float32)
    table[:VOCAB, :D_EMB] = inputs["L0_tok_emb_table"]
    head = np.arange(P) // DH
    q, key = np.arange(P) % QB, np.arange(QB + 2 * PAD)
    inside = (key[None, :] >= q[:, None]) & (key[None, :] <= q[:, None] + 2 * PAD)
    data = {
        "x_ids": ids, "frame_ids": frames, "emb_table_padded": table,
        "proj_w": inputs["L0_tok_proj_w"], "proj_b": inputs["L0_tok_proj_b"],
        "w_qkv": inputs["L0_attn_W_qkv"], "b_qkv": np.asarray(inputs["L0_attn_b_qkv"]).reshape(3, P).T,
        "w_out": inputs["L0_attn_W_out"], "b_out": inputs["L0_attn_b_out"],
        "router_w": inputs["L0_ffn_router_w"], "router_b": inputs["L0_ffn_router_b"],
        "wi": inputs["L0_ffn_Wi"], "wh": inputs["L0_ffn_Wh"], "b_lstm": np.asarray(inputs["L0_ffn_b"]).reshape(E, 4, P).transpose(2, 0, 1),
        "wo": inputs["L0_ffn_Wo"], "bo": inputs["L0_ffn_bo"],
        "dft": dft,
        "vocab_col": np.arange(VOCAB, dtype=np.float32)[:, None],
        "vocab_rows": np.tile(np.arange(VOCAB, dtype=np.float32), (NFFT, 1)),
        "frame_rows": frame_rows,
        "ident": np.eye(P, dtype=np.float32),
        "head_ones": (head[:, None] == head[None, :]).astype(np.float32),
        "band": np.where(inside, 0.0, -1.0e30).astype(np.float32),
        "parity": np.stack([head % 2 == 0, head % 2 == 1], axis=1).astype(np.float32),
        "expert_m8": np.tile(np.arange(E, dtype=np.float32) - E, (P, 1)),
    }
    nc = bacc.Bacc("TRN2", target_bir_lowering=False, num_devices=1)
    arrays, args = {}, []
    for name, a in data.items():
        a = np.ascontiguousarray(a)
        arrays["in_" + name] = a
        args.append(nc.dram_tensor("in_" + name, a.shape, mb.dt.from_np(a.dtype), kind="ExternalInput").ap())
    args.append(nc.dram_tensor("out_dram", (STEPS, SEQ, D), mb.dt.float32, kind="ExternalOutput").ap())
    lm_tower_kernel(nc, *args)
    r = run(nc, [arrays], core_ids=[0])
    return r.results[0]["out_dram"]
```

```python
import concourse.bass as bass
from concourse import mybir
from contextlib import ExitStack


def lm_tower_kernel(nc, x_ids, frame_ids, emb_table, proj_w, proj_b, w_qkv, b_qkv, w_out, b_out,
                    router_w, router_b, wi, wh, b_lstm, wo, bo,
                    dft, vocab_col, vocab_rows, frame_rows, ident_dram, head_ones, band, parity, expert_m8, out):
    f32, f16, bf16, i32 = mybir.dt.float32, mybir.dt.float16, mybir.dt.bfloat16, mybir.dt.int32
    ALU = mybir.AluOpType
    ACT = mybir.ActivationFunctionType
    X = mybir.AxisListType.X

    P = 128
    STEPS, SEQ = x_ids.shape
    VOCAB, D_EMB = 16, 89
    D = w_out.shape[0]
    D_ENC = D - D_EMB
    NFFT, NFREQ = dft.shape[0], dft.shape[2]
    NFR = SEQ // NFFT + 1
    HEADS, DH = 8, 16
    NW = 64
    TF = SEQ - NW
    CH = TF // NW
    PAD = 8
    QB = 16
    KB = QB + 2 * PAD
    NBLK = TF // QB
    HB = NBLK // 2
    E = wi.shape[0]
    K = 2
    TILES = SEQ // P
    EPS = 1e-5
    W_SCALE, V_SCALE = 2.0 ** 6, 2.0 ** 8
    UNSCALE = 1.0 / (W_SCALE * V_SCALE)
    I, F, G, O = 0, 1, 2, 3
    ORDER = (I, G, F, O)
    HI, LO = 0, 1
    NG = 4
    Q_SCALE = 2.0 ** 4
    SP_AT = dict(ids=0, qbd=6, vz=8, rows=28)
    PE_AT = dict(emb=1, xT=3, qkv=4, summary=7, window=8, feature=14, values=18, proj=21, x2T=23,
                 logits=24, maskT=27, bias=29)
    ACT_AT = dict(h=1, xn=2, xT=3, qkv=4, split=5, summary=9, window=11, pr_hi=15, feature=16, xn2=22, x2T=23,
                  choice=25, maskT=27)
    DVE_AT = dict(onehot=0, moments=1, pw=5, q_lo=5, kv_lo=6, v_win=7, w_max=8, s_max=9, s_sub=10, w_sum=11,
                  w_out=12, s_sum=13, s_norm=14, f_max=15, p_lo=16, p_T=16, f_sum=17, f_part=18, attn=19,
                  moments2=21, x_lo=24, choice1=25, choice2=25, weights=26, bias=30)
    MASKS_AT = 29
    XM_AT = 30
    ENC0 = 32

    ctx = ExitStack()
    with ctx:
        def sb(name, shape, dt=f32):
            return ctx.enter_context(nc.sbuf_tensor(name, shape, dt))

        def pb(name, shape, dt=f32):
            return ctx.enter_context(nc.psum_tensor(name, shape, dt))

        def sem(name):
            return ctx.enter_context(nc.semaphore(name))

        wi_sb = sb("wi_sb", [P, E, 2, 4 * P], f16)
        wh_sb = sb("wh_sb", [P, E, 2, 4 * P], f16)
        wo_sb = sb("wo_sb", [P, E, 2, P], f16)
        bias_sb = sb("bias_sb", [P, E, 4])
        C = sb("C", [P, E, K * SEQ])
        Hs = sb("Hs", [P, E, 2, K * SEQ], f16)
        tmp = sb("tmp", [P, 5, K * SEQ])
        masks = sb("masks", [P, 2, K, SEQ], f16)
        xm = sb("xm", [P, 2, K, 2, SEQ], f16)
        xs = sb("xs", [P, 2, 2, SEQ], f16)
        h2 = sb("h2", [P, 2, TILES, D])
        wy = sb("wy", [P, 2, TILES, K, E])
        ids = sb("ids", [VOCAB, SEQ], i32)
        rows = sb("rows", [ENC0 + NFR, SEQ])
        table = sb("table", [ENC0 + NFR, D])
        h_sb = sb("h_sb", [P, TILES, D])
        stats = sb("stats", [P, TILES, 6])
        mv = sb("mv", [P, TILES, 2])
        veps = sb("veps", [P, TILES])
        spare = sb("spare", [P, 1])
        nmr = sb("nmr", [P, TILES])
        rstd = sb("rstd", [P, TILES])
        xn = sb("xn", [P, TILES, D])
        xnT = sb("xnT", [P, SEQ])
        qT = sb("qT", [P, SEQ])
        kw = sb("kw", [P, NW])
        kf = sb("kf", [P, TF + 2 * PAD])
        vw = sb("vw", [P, NW])
        vf = sb("vf", [P, TF + 2 * PAD])
        prod = sb("prod", [P, NW * (CH + 1)])
        ew = sb("ew", [P, NW * (CH + 1)])
        red = sb("red", [P, NW])
        red2 = sb("red2", [P, NW])
        red3 = sb("red3", [P, NW])
        oW = sb("oW", [P, NW])
        qbd = sb("qbd", [P, HEADS * TF])
        vz = sb("vz", [P, P * NBLK])
        vwin = sb("vwin", [P, NBLK * 32])
        pr = sb("pr", [P, NBLK * KB])
        prT = vwin
        wred = sb("wred", [P, 3, NBLK])
        attn = sb("attn", [P, SEQ])
        x32 = xnT
        lg = sb("lg", [P, 8, TILES, E])
        m4 = sb("m4", [P, 10, TILES])
        mk = sb("mk", [P, TILES, K * E])
        mw = sb("mw", [P, TILES, E])
        mrow = ew[0:K * E, 0:SEQ // 2].bitcast(f16)
        wT = attn[0:E, :]
        qperm = attn[:, 0:TF]
        pair16 = lambda ap, n: ap.bitcast(f16).rearrange("p (n v) -> p n v", n=n, v=2)
        qp16, qbd16, vz16 = pair16(qperm, TF), pair16(qbd[:, :], HEADS * TF), pair16(vz[:, :], P * NBLK)
        vp = ew[:, 0:TF + 2 * PAD]
        vp16, pr16, prT16 = pair16(vp, TF + 2 * PAD), pair16(pr[:, :], NBLK * KB), pair16(prT[:, :], NBLK * KB)
        khl = xn[:, :, :].rearrange("p t d -> p (t d)").bitcast(f16)[:, 0:2 * (TF + 2 * PAD)] \
            .rearrange("p (v t) -> p v t", v=2)
        wqkv_sb = sb("wqkv_sb", [P, 3 * D])
        bqkv_sb = sb("bqkv_sb", [P, 3])
        wout_sb = sb("wout_sb", [P, D])
        rw_sb = sb("rw_sb", [P, E])
        rb_sb = sb("rb_sb", [P, E])
        bo_sb = sb("bo_sb", [E, D])
        bout_sb = sb("bout_sb", [1, D])
        ones1 = sb("ones1", [1, P])
        ident = sb("ident", [P, P])
        identb = sb("identb", [P, P], bf16)
        hones = sb("hones", [P, P])
        band_sb = sb("band_sb", [P, KB], f32)
        bandb = sb("bandb", [P, KB], bf16)
        par_sb = sb("par_sb", [P, 2])
        m8_sb = sb("m8_sb", [P, E])
        vcol = sb("vcol", [VOCAB, 1])
        mhalf = sb("mhalf", [P, TILES])
        mones = sb("mones", [P, TILES])

        gates = pb("gates", [P, 2, K * SEQ])
        yp = pb("yp", [P, TILES, D])
        FB = pb("FB", [P, SEQ])
        FA = pb("FA", [P, 2, SEQ])

        stage = C[:, :, :]
        wi_st, wh_st = stage[:, 0:4, :], stage[:, 4:8, :]
        wo_st = xm[:, 0, :, :, :].rearrange("p k v t -> p (k v t)").bitcast(f32)
        NBJ = STEPS * NFR
        fid = tmp[0:NFFT, 2, 512:512 + NBJ].bitcast(i32)
        onehot64 = qbd[0:NFFT, 0:VOCAB * NBJ // 2].bitcast(f16)
        mag = vz[0:NFREQ, 0:VOCAB * NBJ]
        dft_sb = tmp[0:NFFT, 2, 0:2 * NFREQ]
        dft16 = tmp[0:NFFT, 2, 256:256 + 2 * NFREQ].bitcast(f16).rearrange("n (v f) -> n v f", v=2)
        vrow = tmp[0:NFFT, 2, 128:128 + VOCAB]
        pw_sb = tmp[0:NFREQ, 3, 0:VOCAB * D_ENC]
        pbias = tmp[0:D_ENC, 4, 0:1]
        encT = tmp[0:D_ENC, 4, 512:512 + NBJ]
        encA = tmp[:, 4, 128:128 + D_ENC]
        encB = tmp[0:NBJ - P, 4, 256:256 + D_ENC]
        SC = 384
        NSC = VOCAB * NBJ // SC
        sq = tmp[0:NFREQ, 0:2, 0:SC]

        enc_dram = nc.dram_tensor("enc_scratch", (NBJ, D_ENC), f32, kind="Internal").ap()
        mask_dram = nc.dram_tensor("mask_scratch", (STEPS, K * E, SEQ), f16, kind="Internal").ap()

        s_wi_load = sem("s_wi_load")
        s_wh_load = sem("s_wh_load")
        s_wo_load = sem("s_wo_load")
        s_const = sem("s_const")
        s_stft_in = sem("s_stft_in")
        s_zero = sem("s_zero")
        s_whi = sem("s_whi")
        s_wlo = sem("s_wlo")
        s_prep = sem("s_prep")
        s_oh64 = sem("s_oh64")
        s_dft_hi = sem("s_dft_hi")
        s_dft_lo = sem("s_dft_lo")
        s_dft = sem("s_dft")
        s_sq = sem("s_sq")
        s_msq = sem("s_msq")
        s_mag = sem("s_mag")
        s_encT = sem("s_encT")
        s_encT_sb = sem("s_encT_sb")
        s_enc = sem("s_enc")
        s_enc_sb = sem("s_enc_sb")
        s_enc_out = sem("s_enc_out")
        s_czero = sem("s_czero")
        s_mask_in = [sem("s_mask_in0"), sem("s_mask_in1")]
        s_xm = sem("s_xm")
        s_gate = sem("s_gate")
        s_tanh = sem("s_tanh")
        s_u = sem("s_u")
        s_v = sem("s_v")
        s_c = sem("s_c")
        s_tc = sem("s_tc")
        s_h = sem("s_h")
        s_hhi = sem("s_hhi")
        s_hlo = sem("s_hlo")
        s_y = sem("s_y")
        s_yadd = sem("s_yadd")
        s_out = sem("s_out")
        names = """ids enc onehot emb hsb bnst bnag veps rstd xn xnTp xnT qp kp vp q k v qbd vwin vz
            pw sw mw dw ew rw iw ow owr ow_c pf sf mf df ef rf if_ uf S mS dS eS rS iS prT O of0 of1
            mr nmr mr2 nmr2 khi vhi qhi qlo klo vlo pn phi plo cf attn proj h2 bnst2 bnag2 veps2 rstd2 xn2 x2p xhi x32 xlo lgp lg m1 eq1 ix1 im1 k1 l2 m2
            eq2 ix2 im2 k2 dd ed sd w0 w1 wa wb wt mwc mwp mrow wT mout bp h2b wys"""
        S = {n: sem("f_" + n) for n in names.split()}

        def is_zero(b):
            return isinstance(b, int) and b == 0

        def is_one(b):
            return isinstance(b, int) and b == 1

        def run_steps(eng, step):
            step(0, 0, True, False)
            with eng.Fori(0, (STEPS - 2) // 2) as pair:
                step(pair * 2 + 1, 1, False, False)
                step(pair * 2 + 2, 0, False, False)
            step(STEPS - 1, (STEPS - 1) % 2, False, True)

        def row(ap):
            return ap.rearrange("(a n) -> a n", a=1)

        consts = [
            (wqkv_sb[:, :], w_qkv), (bqkv_sb[:, :], b_qkv), (wout_sb[:, :], w_out),
            (rw_sb[:, :], router_w), (rb_sb[:, :], row(router_b).to_broadcast([P, E])), (bo_sb[:, :], bo),
            (bout_sb[:, :], row(b_out)), (ident[:, :], ident_dram), (hones[:, :], head_ones), (band_sb[:, :], band),
            (par_sb[:, :], parity), (m8_sb[:, :], expert_m8), (vcol[:, :], vocab_col),
            (bias_sb[:, :, :], b_lstm),
            (rows[0:ENC0 + NFR, :], frame_rows), (table[0:ENC0 + NFR, :], emb_table),
        ]

        block = ctx.enter_context(nc.Block())

        @block.sync
        def _(sp):
            def load(dst, src, s):
                sp.dma_start(dst, src).then_inc(s, 16)

            load(fid, frame_ids, s_stft_in)
            load(dft_sb, dft.rearrange("n c f -> n (c f)"), s_stft_in)
            load(vrow, vocab_rows, s_stft_in)
            load(pw_sb.rearrange("f (v o) -> f v o", v=VOCAB), proj_w.rearrange("(f v) o -> f v o", v=VOCAB), s_stft_in)
            load(pbias, proj_b.rearrange("(n a) -> n a", a=1), s_stft_in)
            for dst, src in consts:
                load(dst, src, s_const)
            load(wi_st.rearrange("p a (b n) -> p (a b) n", b=2), wi.rearrange("e i n -> i e n"), s_wi_load)
            load(wh_st.rearrange("p a (b n) -> p (a b) n", b=2), wh.rearrange("e i n -> i e n"), s_wh_load)
            load(wo_st.rearrange("p (e n) -> p e n", e=E), wo.rearrange("e i n -> i e n"), s_wo_load)
            sp.wait_ge(s_enc_sb, 2)
            load(enc_dram[0:P, :], encA, s_enc_out)
            load(enc_dram[P:NBJ, :], encB, s_enc_out)
            sp.wait_ge(s_enc_out, 32)

            def front(t, b):
                if t == SP_AT["ids"]:
                    sp_ids(b)
                if t == SP_AT["qbd"]:
                    sp.wait_ge(S["qlo"], b + 1)
                    if not is_zero(b):
                        sp.wait_ge(S["S"], b)
                    for h in range(HEADS):
                        load(qbd[DH * h:DH * h + DH, h * TF:(h + 1) * TF], qperm[DH * h:DH * h + DH, :], S["qbd"])
                if t == SP_AT["vz"]:
                    sp.wait_ge(S["vwin"], b + 1)
                    if not is_zero(b):
                        sp.wait_ge(S["O"], b)
                    for g in range(4):
                        load(vz[32 * g:32 * g + 32, g * KB * NBLK:(g + 1) * KB * NBLK], vwin[32 * g:32 * g + 32, :], S["vz"])
                if t == SP_AT["rows"]:
                    sp.wait_ge(S["mrow"], b + 1)
                    sp.wait_ge(s_enc_out, 32)
                    load(mask_dram[bass.ds(b, 1), :, :].rearrange("a r t -> (a r) t"), mrow[:, :], S["mout"])

            def sp_ids(b):
                if not is_zero(b):
                    sp.wait_ge(S["onehot"], b)
                    sp.wait_ge(S["emb"], b)
                sp.wait_ge(s_enc_out, 32)
                load(ids[:, :], x_ids[bass.ds(b, 1), :].to_broadcast([VOCAB, SEQ]), S["ids"])
                load(table[ENC0:ENC0 + NFR, D_EMB:D],
                     enc_dram.rearrange("(b j) o -> b j o", j=NFR)[bass.ds(b, 1), :, :].rearrange("a j o -> (a j) o"),
                     S["enc"])

            def mask_in(s, e):
                if e == 0:
                    sp.wait_ge(S["mout"], (s + 1) * 16)
                if e >= 2 or not is_zero(s):
                    sp.wait_ge(s_xm, s * E + e - 1)
                sp.wait_ge(s_enc_out, 32)
                src = mask_dram[bass.ds(s, 1), :, :].rearrange("a (k e) t -> (a k) e t", k=K)[:, e, :]
                sp.dma_start(masks[:, e % 2, :, :], src.rearrange("(a k) t -> a k t", a=1)
                             .to_broadcast([P, K, SEQ])).then_inc(s_mask_in[e % 2], 16)

            def store(s, par):
                sp.wait_ge(s_yadd, (s + 1) * (K * E))
                sp.wait_ge(s_enc_out, 32)
                sp.dma_start(out[bass.ds(s, 1), :, :].rearrange("a (t p) d -> p (a t) d", p=P),
                             h2[:, par, :, :]).then_inc(s_out, 16)

            def step(s, par, first, last):
                for t in range(NG * E):
                    e, g = t // NG, t % NG
                    if t == 8 and not first:
                        store(s - 1, 1 - par)
                    if not last:
                        front(t, s + 1)
                    if g == 1 and e < E - 2:
                        mask_in(s, e + 2)
                    if t in (MASKS_AT, MASKS_AT + 1) and not last:
                        mask_in(s + 1, t - MASKS_AT)

            for t in range(NG * E):
                front(t, 0)
            mask_in(0, 0)
            mask_in(0, 1)
            run_steps(sp, step)
            store(STEPS - 1, (STEPS - 1) % 2)
            sp.wait_ge(s_out, 16 * STEPS)

        @block.tensor
        def _(pe):
            mm = nc.tensor.matmul

            pe.wait_ge(s_stft_in, 80)
            pe.wait_ge(s_dft_lo, 1)
            for c in range(NSC):
                if c >= 2:
                    pe.wait_ge(s_sq, 2 * (c - 1))
                if c % 2 == 0:
                    pe.wait_ge(s_oh64, c // 2 + 1)
                for r in range(2):
                    for v in (HI, LO):
                        last = mm(gates[0:NFREQ, c % 2, r * SEQ:r * SEQ + SC], dft16[:, v, r * NFREQ:(r + 1) * NFREQ],
                                  onehot64[:, c * SC:(c + 1) * SC], start=(v == HI), stop=(v == LO))
                    last.then_inc(s_dft, 1)
            pe.wait_ge(s_mag, 1)
            for v in range(VOCAB):
                last = mm(FA[0:D_ENC, 0, 0:NBJ], pw_sb[:, v * D_ENC:(v + 1) * D_ENC], mag[:, v * NBJ:(v + 1) * NBJ],
                          start=(v == 0), stop=(v == VOCAB - 1))
            last.then_inc(s_encT, 1)
            pe.wait_ge(s_const, 16 * len(consts))
            pe.wait_ge(s_encT_sb, 1)
            for (c0, n, at) in ((0, P, 0), (P, NBJ - P, 64)):
                last = nc.tensor.transpose(FA[0:n, 1, at:at + D_ENC], encT[:, c0:c0 + n], ident[0:D_ENC, 0:D_ENC])
            last.then_inc(s_enc, 1)

            def front(t, b):
                b1 = b + 1
                if t == PE_AT["emb"]:
                    pe.wait_ge(S["onehot"], b1)
                    pe.wait_ge(S["enc"], 16 * b1)
                    for i in range(TILES):
                        last = mm(FB[:, i * D:(i + 1) * D], rows[:, i * P:(i + 1) * P], table[:, :],
                                  start=True, stop=True)
                    last.then_inc(S["emb"], 1)
                if t == PE_AT["xT"]:
                    pe.wait_ge(S["xn"], b1)
                    pe.wait_ge(S["hsb"], b1)
                    for i in range(TILES):
                        last = nc.tensor.transpose(FB[:, i * P:(i + 1) * P], xn[:, i, :], ident[:, :])
                    last.then_inc(S["xnTp"], 1)
                if t == PE_AT["qkv"]:
                    pe.wait_ge(S["xnT"], b1)
                    for j, dst, s in ((0, FA[:, 0, :], "qp"), (1, FA[:, 1, :], "kp"), (2, FB[:, :], "vp")):
                        mm(dst, wqkv_sb[:, j * D:(j + 1) * D], xnT[:, :], start=True, stop=True).then_inc(S[s], 1)
                if t == PE_AT["summary"]:
                    pe.wait_ge(S["pw"], b1)
                    pe.wait_ge(S["v"], b1)
                    mm(FB[:, :], hones[:, :], prod[:, :], start=True, stop=True).then_inc(S["sw"], 1)
                if t == PE_AT["window"]:
                    pe.wait_ge(S["qbd"], 128 * b1)
                    pe.wait_ge(S["klo"], b1)
                    for r in range(2):
                        mm(FA[:, r, 0:HB * KB], identb[:, :],
                           bandb[:, :].rearrange("p (a k) -> p a k", a=1).to_broadcast([P, HB, KB]),
                           start=True, stop=False, skip_group_check=True)
                        for jj in range(HB):
                            j = r * HB + jj
                            for qv, kv in ((HI, HI), (HI, LO), (LO, HI)):
                                last = mm(FA[:, r, jj * KB:(jj + 1) * KB], qbd16[:, j::NBLK, qv],
                                          khl[:, kv, j * QB:j * QB + KB], start=False,
                                          stop=(jj == HB - 1 and qv == LO), skip_group_check=True)
                    last.then_inc(S["S"], 1)
                if t == PE_AT["feature"]:
                    pe.wait_ge(S["pf"], b1)
                    mm(FB[:, 0:TF], hones[:, :], prod[:, 0:TF], start=True, stop=True).then_inc(S["sf"], 1)
                if t == PE_AT["values"]:
                    pe.wait_ge(S["prT"], b1)
                    pe.wait_ge(S["vz"], 64 * b1)
                    for j in range(NBLK):
                        for vv, pv in ((HI, HI), (HI, LO), (LO, HI)):
                            last = mm(FA[:, j // HB, (j % HB) * KB:(j % HB + 1) * KB], vz16[:, j::NBLK, vv],
                                      prT16[:, j * KB:(j + 1) * KB, pv], start=(vv == HI and pv == HI), stop=(vv == LO))
                    last.then_inc(S["O"], 1)
                if t == PE_AT["proj"]:
                    pe.wait_ge(S["attn"], b1)
                    for i in range(TILES):
                        mm(FB[:, i * D:(i + 1) * D], attn[:, i * P:(i + 1) * P], wout_sb[:, :], start=True, stop=False)
                        last = mm(FB[:, i * D:(i + 1) * D], ones1[:, :], bout_sb[:, :], start=False, stop=True)
                    last.then_inc(S["proj"], 1)
                if t == PE_AT["x2T"]:
                    pe.wait_ge(S["xn2"], b1)
                    for i in range(TILES):
                        last = nc.tensor.transpose(FB[:, i * P:(i + 1) * P], xn[:, i, :], ident[:, :])
                    last.then_inc(S["x2p"], 1)
                if t == PE_AT["logits"]:
                    pe.wait_ge(S["x32"], b1)
                    pe.wait_ge(S["attn"], b1)
                    for i in range(TILES):
                        last = mm(FA[:, 1, i * E:(i + 1) * E], x32[:, i * P:(i + 1) * P], rw_sb[:, :], start=True, stop=True)
                    last.then_inc(S["lgp"], 1)
                if t == PE_AT["maskT"]:
                    pe.wait_ge(S["mwc"], b1)
                    pe.wait_ge(S["xlo"], b1)
                    for i in range(TILES):
                        nc.tensor.transpose(FB[0:K * E, i * P:(i + 1) * P], mk[:, i, :], ident[:, :])
                    for i in range(TILES):
                        last = nc.tensor.transpose(FA[0:E, 1, i * P:(i + 1) * P], mw[:, i, :], ident[:, :])
                    last.then_inc(S["mwp"], 1)
                if t == PE_AT["bias"]:
                    pe.wait_ge(S["wT"], b1)
                    for i in range(TILES):
                        last = mm(FA[:, 0, i * D:(i + 1) * D], wT[:, i * P:(i + 1) * P], bo_sb[:, :], start=True, stop=True)
                    last.then_inc(S["bp"], 1)

            def unit_gate(s, e, g, first):
                gate = ORDER[g]
                slot = g % 2
                if not (first and e == 0 and g < 2):
                    pe.wait_ge(s_tanh, s * (E * NG) + e * NG + g - 1)
                if g == 0:
                    pe.wait_ge(s_xm, s * E + e + 1)
                    if not first:
                        pe.wait_ge(s_hlo, s * E + e - E + 1)
                parts = [(wi_sb, lambda k, v: xm[:, e % 2, k, v, :])]
                if not first:
                    parts.append((wh_sb, lambda k, v: Hs[:, e, v, k * SEQ:(k + 1) * SEQ]))
                seq = []
                for w, mov in parts:
                    for wpart, vpart in ((HI, HI), (HI, LO), (LO, HI)):
                        for k in range(K):
                            seq.append((w[:, e, wpart, gate * P:(gate + 1) * P], mov(k, vpart), k))
                for n, (w, v, k) in enumerate(seq):
                    last = mm(gates[:, slot, k * SEQ:(k + 1) * SEQ], w, v, start=(n < K), stop=(n >= len(seq) - K))
                last.then_inc(s_gate, 1)

            def unit_y(s, e, k, yfirst):
                pe.wait_ge(s_hlo, s * E + e + 1)
                if not yfirst:
                    pe.wait_ge(s_yadd, s * (E * K) + e * K + k)
                for i in range(TILES):
                    tok = slice(k * SEQ + i * P, k * SEQ + (i + 1) * P)
                    mm(yp[:, i, :], Hs[:, e, HI, tok], wo_sb[:, e, HI, :], start=True, stop=False)
                    mm(yp[:, i, :], Hs[:, e, HI, tok], wo_sb[:, e, LO, :], start=False, stop=False)
                    last = mm(yp[:, i, :], Hs[:, e, LO, tok], wo_sb[:, e, HI, :], start=False, stop=True)
                last.then_inc(s_y, 1)

            def step(s, par, first, last):
                for t in range(NG * E):
                    e, g = t // NG, t % NG
                    unit_gate(s, e, g, first)
                    if g in (1, 3):
                        if e >= 2:
                            unit_y(s, e - 2, g // 2, first and e == 2 and g == 1)
                        elif not first:
                            unit_y(s - 1, e - 2 + E, g // 2, False)
                    if not last:
                        front(t, s + 1)

            pe.wait_ge(s_const, 16 * len(consts))
            pe.wait_ge(s_zero, 1)
            pe.wait_ge(s_prep, 4)
            for t in range(NG * E):
                front(t, 0)
            pe.wait_ge(s_wlo, 8)
            run_steps(pe, step)
            for e in (E - 2, E - 1):
                for k in range(K):
                    unit_y(STEPS - 1, e, k, False)

        @block.scalar
        def _(act):
            A = nc.scalar.activation
            act.wait_ge(s_stft_in, 80)
            A(dft16[:, HI, :], dft_sb, ACT.Copy, scale=V_SCALE).then_inc(s_dft_hi, 1)
            for c in range(NSC):
                act.wait_ge(s_dft, 2 * c + 2)
                if c >= 1:
                    act.wait_ge(s_msq, c)
                for r in range(2):
                    A(sq[:, r, :], gates[0:NFREQ, c % 2, r * SEQ:r * SEQ + SC], ACT.Square,
                      scale=1.0 / V_SCALE).then_inc(s_sq, 1)
            act.wait_ge(s_msq, NSC)
            A(mag, mag, ACT.Sqrt).then_inc(s_mag, 1)

            def front(t, b):
                b1 = b + 1
                if t == ACT_AT["h"]:
                    act.wait_ge(S["emb"], b1)
                    if not is_zero(b):
                        act.wait_ge(S["h2"], b)
                    A(h_sb[:, :, :].rearrange("p t d -> p (t d)"), FB[:, :], ACT.Copy).then_inc(S["hsb"], 1)
                for at, ready, src, dst in (("xn", "nmr", lambda i: h_sb[:, i, :], "xn"),
                                            ("xn2", "nmr2", lambda i: h2[:, par_of(b), i, :], "xn2")):
                    if t == ACT_AT[at]:
                        act.wait_ge(S[ready], b1)
                        if at == "xn":
                            act.wait_ge(S["hsb"], b1)
                        for i in range(TILES):
                            last = A(xn[:, i, :], src(i), ACT.Identity, bias=nmr[:, i:i + 1], scale=rstd[:, i:i + 1])
                        last.then_inc(S[dst], 1)
                if t == ACT_AT["xT"]:
                    act.wait_ge(S["xnTp"], b1)
                    A(xnT[:, :], FB[:, :], ACT.Copy).then_inc(S["xnT"], 1)
                if t == ACT_AT["qkv"]:
                    act.wait_ge(s_prep, 4)
                    act.wait_ge(S["qp"], b1)
                    if not is_zero(b):
                        act.wait_ge(S["S"], b)
                    A(qT[:, :], FA[:, 0, :], ACT.Identity, bias=bqkv_sb[:, 0:1], scale=DH ** -0.5).then_inc(S["q"], 1)
                    act.wait_ge(S["q"], b1)
                    if not is_zero(b):
                        act.wait_ge(S["bp"], b)
                    A(qp16[:, :, HI].rearrange("p (q j) -> p j q", j=NBLK),
                      qT[:, NW:SEQ].rearrange("p (j q) -> p j q", j=NBLK), ACT.Copy, scale=Q_SCALE).then_inc(S["qhi"], 1)
                    act.wait_ge(S["kp"], b1)
                    A(kw[:, :], FA[:, 1, 0:NW], ACT.Identity, bias=bqkv_sb[:, 1:2])
                    A(kf[:, PAD:PAD + TF], FA[:, 1, NW:SEQ], ACT.Identity, bias=bqkv_sb[:, 1:2]).then_inc(S["k"], 1)
                    act.wait_ge(S["vp"], b1)
                    A(vw[:, :], FB[:, 0:NW], ACT.Identity, bias=bqkv_sb[:, 2:3])
                    A(vf[:, PAD:PAD + TF], FB[:, NW:SEQ], ACT.Identity, bias=bqkv_sb[:, 2:3]).then_inc(S["v"], 1)
                if t == ACT_AT["split"]:
                    if not is_zero(b):
                        act.wait_ge(S["mout"], 16 * b)
                    act.wait_ge(S["k"], b1)
                    A(khl[:, HI, :], kf[:, :], ACT.Copy, scale=Q_SCALE).then_inc(S["khi"], 1)
                    act.wait_ge(S["v"], b1)
                    A(vp16[:, :, HI], vf[:, :], ACT.Copy, scale=Q_SCALE).then_inc(S["vhi"], 1)
                if t == ACT_AT["summary"]:
                    act.wait_ge(S["dw"], b1)
                    A(ew[:, :], prod[:, :], ACT.Exp).then_inc(S["ew"], 1)
                if t == ACT_AT["window"]:
                    act.wait_ge(S["dS"], b1)
                    A(pr[:, :], pr[:, :], ACT.Exp, scale=1.0 / (Q_SCALE * Q_SCALE)).then_inc(S["eS"], 1)
                if t == ACT_AT["pr_hi"]:
                    act.wait_ge(S["pn"], b1)
                    A(pr16[:, :, HI], vwin[:, :], ACT.Copy, scale=V_SCALE).then_inc(S["phi"], 1)
                if t == ACT_AT["feature"]:
                    act.wait_ge(S["df"], b1)
                    A(ew[:, 0:TF], prod[:, 0:TF], ACT.Exp).then_inc(S["ef"], 1)
                if t == ACT_AT["x2T"]:
                    act.wait_ge(S["x2p"], b1)
                    A(x32[:, :], FB[:, :], ACT.Copy).then_inc(S["x32"], 1)
                    A(xs[:, par_of(b), HI, :], FB[:, :], ACT.Copy, scale=V_SCALE).then_inc(S["xhi"], 1)
                if t == ACT_AT["choice"]:
                    act.wait_ge(S["dd"], b1)
                    A(m4[:, 6, :], m4[:, 5, :], ACT.Exp).then_inc(S["ed"], 1)
                if t == ACT_AT["maskT"]:
                    act.wait_ge(S["mwp"], b1)
                    if not is_zero(b):
                        act.wait_ge(S["mout"], 16 * b)
                    A(mrow[:, :], FB[0:K * E, :], ACT.Copy).then_inc(S["mrow"], 1)
                    A(wT[:, :], FA[0:E, 1, :], ACT.Copy).then_inc(S["wT"], 1)

            def gate_tanh(s, e, g, first):
                gate = ORDER[g]
                act.wait_ge(s_gate, s * (E * NG) + e * NG + g + 1)
                if not (first and e == 0):
                    if gate == O:
                        act.wait_ge(s_hlo, s * E + e)
                    else:
                        act.wait_ge(s_c, s * E + e)
                A(tmp[:, gate, :], gates[:, g % 2, :], ACT.Tanh, bias=bias_sb[:, e, gate:gate + 1],
                  scale=UNSCALE).then_inc(s_tanh, 1)

            def cell_tanh(s, e):
                act.wait_ge(s_c, s * E + e + 1)
                A(tmp[:, 4, :], C[:, e, :], ACT.Tanh, scale=0.5).then_inc(s_tc, 1)

            def split_hi(s, e):
                act.wait_ge(s_h, s * E + e + 1)
                A(Hs[:, e, HI, :], tmp[:, O, :], ACT.Copy, scale=V_SCALE).then_inc(s_hhi, 1)

            def step(s, par, first, last):
                for t in range(NG * E):
                    e, g = t // NG, t % NG
                    gate_tanh(s, e, g, first)
                    if g == 0 and e:
                        split_hi(s, e - 1)
                    elif g == 0 and not first:
                        split_hi(s - 1, E - 1)
                    if g == 3:
                        cell_tanh(s, e)
                    if not last:
                        front(t, s + 1)

            par_of = lambda b: PAR[0]
            PAR = [0]

            def split_w_hi(src, dst, f, s_load):
                    act.wait_ge(s_load, 16)
                    v = src.rearrange("p a (b n) -> p (a b) n", b=2)
                    for c0, c1, half in ((0, 2, 0.5), (2, 3, 1.0), (3, 4, 0.5)):
                        A(dst[:, :, HI, c0 * P:c1 * P], v[:, :, c0 * P:c1 * P], ACT.Copy,
                          scale=W_SCALE * f * half).then_inc(s_whi, 1)

            split_w_hi(wi_st, wi_sb, 1.0, s_wi_load)
            act.wait_ge(s_encT, 1)
            A(encT, FA[0:D_ENC, 0, 0:NBJ], ACT.Identity, bias=pbias).then_inc(s_encT_sb, 1)
            act.wait_ge(s_enc, 1)
            A(encA, FA[:, 1, 0:D_ENC], ACT.Copy).then_inc(s_enc_sb, 1)
            A(encB, FA[0:NBJ - P, 1, 64:64 + D_ENC], ACT.Copy).then_inc(s_enc_sb, 1)
            act.wait_ge(s_const, 16 * len(consts))
            split_w_hi(wh_st, wh_sb, 0.5, s_wh_load)
            act.wait_ge(s_wo_load, 16)
            A(wo_sb[:, :, HI, :], wo_st.rearrange("p (e n) -> p e n", e=E), ACT.Copy,
              scale=W_SCALE * 0.5).then_inc(s_whi, 1)
            for t in range(NG * E):
                front(t, 0)

            def step_p(s, par, first, last):
                PAR[0] = 1 - par
                step(s, par, first, last)

            run_steps(act, step_p)
            split_hi(STEPS - 1, E - 1)

        @block.vector
        def _(dve):
            V = nc.vector
            TT, TS, STT = V.tensor_tensor, V.tensor_scalar, V.scalar_tensor_tensor
            dve.wait_ge(s_stft_in, 80)
            NV = VOCAB // 3 + 1
            for v0 in range(0, VOCAB, NV):
                v1 = min(VOCAB, v0 + NV)
                TT(onehot64[:, v0 * NBJ:v1 * NBJ].rearrange("p (v n) -> p v n", n=NBJ),
                   fid.rearrange("p (a n) -> p a n", a=1).to_broadcast([NFFT, v1 - v0, NBJ]),
                   vrow[:, v0:v1].rearrange("p (v a) -> p v a", a=1).to_broadcast([NFFT, v1 - v0, NBJ]),
                   ALU.is_equal).then_inc(s_oh64, 1)
                if v0 == 0:
                    dve.wait_ge(s_dft_hi, 1)
                    STT(out=dft16[:, LO, :], in0=dft_sb, scalar=V_SCALE, in1=dft16[:, HI, :],
                        op0=ALU.mult, op1=ALU.subtract).then_inc(s_dft_lo, 1)
            V.memset(ones1[:, :], 1.0).then_inc(s_prep, 1)
            dve.wait_ge(s_const, 16 * len(consts))
            V.tensor_copy(identb[:, :], ident[:, :]).then_inc(s_prep, 1)
            V.tensor_copy(bandb[:, :], band_sb[:, :]).then_inc(s_prep, 1)
            TS(bqkv_sb[:, 0:1], bqkv_sb[:, 0:1], DH ** -0.5, None, ALU.mult)
            TS(bias_sb[:, :, I:F + 1], bias_sb[:, :, I:F + 1], 0.5, None, ALU.mult)
            TS(bias_sb[:, :, O:O + 1], bias_sb[:, :, O:O + 1], 0.5, None, ALU.mult).then_inc(s_prep, 1)
            for c in range(NSC):
                dve.wait_ge(s_sq, 2 * c + 2)
                TT(mag[:, c * SC:(c + 1) * SC], sq[:, 0, :], sq[:, 1, :], ALU.add).then_inc(s_msq, 1)

            def split_w_lo(a, b):
                parts = [(src.rearrange("p a (b n) -> p (a b) n", b=2)[:, :, c0 * P:c1 * P],
                          dst[:, :, :, c0 * P:c1 * P], W_SCALE * f * half)
                         for src, dst, f in ((wi_st, wi_sb, 1.0), (wh_st, wh_sb, 0.5))
                         for c0, c1, half in ((0, 2, 0.5), (2, 3, 1.0), (3, 4, 0.5))]
                parts.append((wo_st.rearrange("p (e n) -> p e n", e=E), wo_sb[:, :, :, :], W_SCALE * 0.5))
                for n, (src, dst, scale) in list(enumerate(parts))[a:b]:
                    dve.wait_ge(s_whi, n + 1)
                    STT(out=dst[:, :, LO, :], in0=src, scalar=scale, in1=dst[:, :, HI, :],
                        op0=ALU.mult, op1=ALU.subtract).then_inc(s_wlo, 1)

            def wait(name, n):
                dve.wait_ge(S[name], n)

            def norm_stats(src, names):
                for i in range(TILES):
                    last = V.bn_stats(stats[:, i, :], src(i))
                last.then_inc(S[names[0]], 1)
                return last

            def c3(ap, n):
                return ap.rearrange("p (n c) -> p n c", n=n)

            def bc(ap, n, c):
                return ap.rearrange("p (n a) -> p n a", a=1).to_broadcast([P, n, c])

            def front(t, b, q):
                b1 = b + 1
                if t == DVE_AT["onehot"]:
                    wait("ids", 16 * b1)
                    if not is_zero(b):
                        wait("emb", b)
                    TS(rows[0:VOCAB, :], ids[:, :], vcol[:, 0:1], None, ALU.is_equal).then_inc(S["onehot"], 1)
                if t == DVE_AT["moments"]:
                    wait("hsb", b1)
                    norm_stats(lambda i: h_sb[:, i, :], ("bnst",))
                    wait("bnst", b1)
                    V.memset(spare[:, :], 0.0)
                    for i in range(TILES):
                        last = V.bn_aggr(mv[:, i, :], stats[:, i, :])
                    last.then_inc(S["bnag"], 1)
                    wait("bnag", b1)
                    TS(veps[:, :], mv[:, :, 1], EPS, None, ALU.add).then_inc(S["veps"], 1)
                if t == DVE_AT["pw"]:
                    wait("q", b1)
                    wait("k", b1)
                    p3 = c3(prod[:, :], NW)
                    TT(p3[:, :, 0], qT[:, 0:NW], kw[:, :], ALU.mult)
                    TT(p3[:, :, 1:CH + 1], bc(qT[:, 0:NW], NW, CH), c3(kf[:, PAD:PAD + TF], NW), ALU.mult).then_inc(S["pw"], 1)
                if t == DVE_AT["q_lo"]:
                    wait("qhi", b1)
                    STT(out=qp16[:, :, LO].rearrange("p (q j) -> p j q", j=NBLK),
                        in0=qT[:, NW:SEQ].rearrange("p (j q) -> p j q", j=NBLK), scalar=Q_SCALE,
                        in1=qp16[:, :, HI].rearrange("p (q j) -> p j q", j=NBLK),
                        op0=ALU.mult, op1=ALU.subtract).then_inc(S["qlo"], 1)
                if t == DVE_AT["kv_lo"]:
                    wait("khi", b1)
                    STT(out=khl[:, LO, :], in0=kf[:, :], scalar=Q_SCALE, in1=khl[:, HI, :],
                        op0=ALU.mult, op1=ALU.subtract).then_inc(S["klo"], 1)
                    wait("vhi", b1)
                    STT(out=vp16[:, :, LO], in0=vf[:, :], scalar=Q_SCALE, in1=vp16[:, :, HI],
                        op0=ALU.mult, op1=ALU.subtract).then_inc(S["vlo"], 1)
                if t == DVE_AT["v_win"]:
                    if not is_zero(b):
                        wait("O", b)
                    wait("vlo", b1)
                    win = bass.AP(tensor=vp.tensor, offset=vp.offset, ap=[list(vp.ap[0]), [QB, NBLK], [1, KB]])
                    V.transpose(vwin[:, :].rearrange("p (c j) -> p j c", j=NBLK), win).then_inc(S["vwin"], 1)
                if t == DVE_AT["w_max"]:
                    wait("sw", b1)
                    s3 = c3(FB[:, :], NW)
                    V.tensor_reduce(red[:, :], s3, axis=X, op=ALU.max).then_inc(S["mw"], 1)
                    wait("mw", b1)
                    TT(c3(prod[:, :], NW), s3, bc(red[:, :], NW, CH + 1), ALU.subtract).then_inc(S["dw"], 1)
                if t == DVE_AT["w_sum"]:
                    wait("ew", b1)
                    e3 = c3(ew[:, :], NW)
                    V.tensor_reduce(red[:, :], e3, axis=X, op=ALU.add).then_inc(S["rw"], 1)
                    wait("rw", b1)
                    V.reciprocal(red2[:, :], red[:, :]).then_inc(S["iw"], 1)
                    p3 = c3(prod[:, :], NW)
                    TT(p3[:, :, 0], e3[:, :, 0], vw[:, :], ALU.mult)
                    TT(p3[:, :, 1:CH + 1], e3[:, :, 1:CH + 1], c3(vf[:, PAD:PAD + TF], NW), ALU.mult).then_inc(S["ow"], 1)
                if t == DVE_AT["w_out"]:
                    wait("ow", b1)
                    p3 = c3(prod[:, :], NW)
                    V.tensor_reduce(red3[:, :], p3, axis=X, op=ALU.add).then_inc(S["owr"], 1)
                    wait("owr", b1)
                    wait("iw", b1)
                    TT(oW[:, :], red3[:, :], red2[:, :], ALU.mult).then_inc(S["ow_c"], 1)
                    wait("ow_c", b1)
                    TT(c3(prod[:, 0:TF], NW), c3(qT[:, NW:SEQ], NW), bc(oW[:, :], NW, CH), ALU.mult).then_inc(S["pf"], 1)
                if t == DVE_AT["s_max"]:
                    wait("S", b1)
                    s4 = FA[:, :, 0:HB * KB].rearrange("p r (j k) -> p r j k", k=KB)
                    V.tensor_reduce(wred[:, 0, :].rearrange("p (r j) -> p r j", r=2), s4, axis=X, op=ALU.max).then_inc(S["mS"], 1)
                if t == DVE_AT["s_sub"]:
                    wait("mS", b1)
                    s4 = FA[:, :, 0:HB * KB].rearrange("p r (j k) -> p r j k", k=KB)
                    TT(pr[:, :].rearrange("p (r j k) -> p r j k", r=2, k=KB), s4,
                       wred[:, 0, :].rearrange("p (r j a) -> p r j a", r=2, a=1).to_broadcast([P, 2, HB, KB]),
                       ALU.subtract).then_inc(S["dS"], 1)
                if t == DVE_AT["f_max"]:
                    wait("sf", b1)
                    s3 = c3(FB[:, 0:TF], NW)
                    V.tensor_reduce(red[:, :], s3, axis=X, op=ALU.max).then_inc(S["mf"], 1)
                    wait("mf", b1)
                    TT(c3(prod[:, 0:TF], NW), s3, bc(red[:, :], NW, CH), ALU.subtract).then_inc(S["df"], 1)
                if t == DVE_AT["s_sum"]:
                    wait("eS", b1)
                    V.tensor_reduce(wred[:, 1, :], c3(pr[:, :], NBLK), axis=X, op=ALU.add).then_inc(S["rS"], 1)
                    wait("rS", b1)
                    V.reciprocal(wred[:, 2, :], wred[:, 1, :]).then_inc(S["iS"], 1)
                if t == DVE_AT["s_norm"]:
                    wait("iS", b1)
                    wait("vz", 64 * b1)
                    TT(c3(vwin[:, :], NBLK), c3(pr[:, :], NBLK), bc(wred[:, 2, :], NBLK, KB), ALU.mult).then_inc(S["pn"], 1)
                if t == DVE_AT["p_lo"]:
                    wait("phi", b1)
                    STT(out=pr16[:, :, LO], in0=vwin[:, :], scalar=V_SCALE, in1=pr16[:, :, HI],
                        op0=ALU.mult, op1=ALU.subtract).then_inc(S["plo"], 1)
                if t == DVE_AT["p_T"]:
                    wait("plo", b1)
                    V.transpose(prT[:, :], pr[:, :]).then_inc(S["prT"], 1)
                if t == DVE_AT["f_sum"]:
                    wait("ef", b1)
                    e3 = c3(ew[:, 0:TF], NW)
                    V.tensor_reduce(red[:, :], e3, axis=X, op=ALU.add).then_inc(S["rf"], 1)
                    wait("rf", b1)
                    V.reciprocal(red2[:, :], red[:, :]).then_inc(S["if_"], 1)
                if t == DVE_AT["f_part"]:
                    e3 = c3(ew[:, 0:TF], NW)
                    wait("if_", b1)
                    TT(red3[:, :], oW[:, :], red2[:, :], ALU.mult).then_inc(S["uf"], 1)
                    wait("uf", b1)
                    V.tensor_copy(attn[:, 0:NW], oW[:, :])
                    TT(c3(attn[:, NW:SEQ], NW), e3, bc(red3[:, :], NW, CH), ALU.mult).then_inc(S["cf"], 1)
                    wait("cf", b1)
                if t == DVE_AT["attn"]:
                    wait("O", b1)
                    for par2 in range(2):
                        for r in range(2):
                            o3 = FA[:, r, 0:HB * KB].rearrange("p (j c q) -> p j c q", c=2, q=QB)[:, :, par2, :]
                            a3 = attn[:, NW + r * HB * QB:NW + (r + 1) * HB * QB].rearrange("p (j q) -> p j q", q=QB)
                            last = STT(out=a3, in0=o3, scalar=par_sb[:, par2:par2 + 1], in1=a3, op0=ALU.mult, op1=ALU.add)
                        if par2 == 0:
                            last.then_inc(S["of0"], 1)
                            wait("of0", b1)
                    last.then_inc(S["attn"], 1)
                if t == DVE_AT["moments2"]:
                    wait("proj", b1)
                    if not (is_zero(b) or is_one(b)):
                        dve.wait_ge(s_out, 16 * (b - 1))
                    TT(h2[:, q, :, :].rearrange("p t d -> p (t d)"), FB[:, :],
                       h_sb[:, :, :].rearrange("p t d -> p (t d)"), ALU.add).then_inc(S["h2"], 1)
                    wait("h2", b1)
                    norm_stats(lambda i: h2[:, q, i, :], ("bnst2",))
                    wait("bnst2", b1)
                    V.memset(spare[:, :], 0.0)
                    for i in range(TILES):
                        last = V.bn_aggr(mv[:, i, :], stats[:, i, :])
                    last.then_inc(S["bnag2"], 1)
                    wait("bnag2", b1)
                    TS(veps[:, :], mv[:, :, 1], EPS, None, ALU.add).then_inc(S["veps2"], 1)
                if t == DVE_AT["x_lo"]:
                    wait("xhi", b1)
                    STT(out=xs[:, q, LO, :], in0=FB[:, :], scalar=V_SCALE, in1=xs[:, q, HI, :],
                        op0=ALU.mult, op1=ALU.subtract).then_inc(S["xlo"], 1)
                L, EQ, IX, K1, L2, EQ2, IX2, K2 = (lg[:, i, :, :] for i in range(8))
                M = lambda i: m4[:, i, :]
                Mb = lambda i: m4[:, i, :].rearrange("p (t a) -> p t a", a=1).to_broadcast([P, TILES, E])
                e8 = m8_sb[:, :].rearrange("p (a e) -> p a e", a=1).to_broadcast([P, TILES, E])
                if t == DVE_AT["choice1"]:
                    wait("lgp", b1)
                    TT(L, FA[:, 1, 0:TILES * E].rearrange("p (t e) -> p t e", e=E),
                       rb_sb[:, :].rearrange("p (a e) -> p a e", a=1).to_broadcast([P, TILES, E]), ALU.add).then_inc(S["lg"], 1)
                    wait("lg", b1)
                    V.tensor_reduce(M(0), L, axis=X, op=ALU.max).then_inc(S["m1"], 1)
                    wait("m1", b1)
                    TT(EQ, L, Mb(0), ALU.is_ge).then_inc(S["eq1"], 1)
                    wait("eq1", b1)
                    TT(IX, EQ, e8, ALU.mult).then_inc(S["ix1"], 1)
                    wait("ix1", b1)
                    V.tensor_reduce(M(1), IX, axis=X, op=ALU.min).then_inc(S["im1"], 1)
                if t == DVE_AT["choice2"]:
                    wait("im1", b1)
                    TT(K1, e8, Mb(1), ALU.is_equal).then_inc(S["k1"], 1)
                    wait("k1", b1)
                    STT(out=L2, in0=K1, scalar=-3.0e38, in1=L, op0=ALU.mult, op1=ALU.add).then_inc(S["l2"], 1)
                    wait("l2", b1)
                    V.tensor_reduce(M(2), L2, axis=X, op=ALU.max).then_inc(S["m2"], 1)
                    wait("m2", b1)
                    TT(M(5), M(2), M(0), ALU.subtract).then_inc(S["dd"], 1)
                    TT(EQ2, L2, Mb(2), ALU.is_ge).then_inc(S["eq2"], 1)
                    wait("eq2", b1)
                    TT(IX2, EQ2, e8, ALU.mult).then_inc(S["ix2"], 1)
                    wait("ix2", b1)
                    V.tensor_reduce(M(3), IX2, axis=X, op=ALU.min).then_inc(S["im2"], 1)
                    wait("im2", b1)
                    TT(K2, e8, Mb(3), ALU.is_equal).then_inc(S["k2"], 1)
                if t == DVE_AT["weights"]:
                    wait("ed", b1)
                    TS(M(7), M(6), 1.0, None, ALU.add).then_inc(S["sd"], 1)
                    wait("sd", b1)
                    V.reciprocal(M(8), M(7)).then_inc(S["w0"], 1)
                    wait("w0", b1)
                    TT(M(9), M(8), M(6), ALU.mult).then_inc(S["w1"], 1)
                    wait("w1", b1)
                    wait("k2", b1)
                    TT(IX, K1, Mb(8), ALU.mult).then_inc(S["wa"], 1)
                    TT(IX2, K2, Mb(9), ALU.mult).then_inc(S["wb"], 1)
                    V.tensor_copy(mk[:, :, 0:E], K1)
                    V.tensor_copy(mk[:, :, E:2 * E], K2)
                    wait("wb", b1)
                    TT(mw[:, :, :], IX, IX2, ALU.add).then_inc(S["mwc"], 1)
                    TS(wy[:, q, :, 0, :], IX, UNSCALE, None, ALU.mult)
                    TS(wy[:, q, :, 1, :], IX2, UNSCALE, None, ALU.mult).then_inc(S["wys"], 1)
                if t == DVE_AT["bias"]:
                    wait("bp", b1)
                    flat = h2[:, q, :, :].rearrange("p t d -> p (t d)")
                    TT(flat, flat, FA[:, 0, :], ALU.add).then_inc(S["h2b"], 1)

            def masked_input(s, e, par, xfirst):
                dve.wait_ge(s_mask_in[e % 2], s * (16 * E // 2) + 16 * (e // 2 + 1))
                if e == 0:
                    dve.wait_ge(S["xlo"], s + 1)
                if not xfirst:
                    dve.wait_ge(s_gate, s * (E * NG) + (e - 1) * NG)
                xv = xs[:, par, :, :].rearrange("p (a v) t -> p a v t", a=1).to_broadcast([P, K, 2, SEQ])
                mv_ = masks[:, e % 2, :, :].rearrange("p k (a t) -> p k a t", a=1).to_broadcast([P, K, 2, SEQ])
                TT(xm[:, e % 2, :, :, :], xv, mv_, ALU.mult).then_inc(s_xm, 1)

            def hidden(s, e):
                dve.wait_ge(s_tc, s * E + e + 1)
                dve.wait_ge(s_tanh, s * (E * NG) + e * NG + 4)
                STT(out=tmp[:, O, :], in0=tmp[:, O, :], scalar=1.0, in1=tmp[:, 4, :],
                    op0=ALU.add, op1=ALU.mult).then_inc(s_h, 1)

            def hidden_lo(s, e):
                dve.wait_ge(s_hhi, s * E + e + 1)
                STT(out=Hs[:, e, LO, :], in0=tmp[:, O, :], scalar=V_SCALE, in1=Hs[:, e, HI, :],
                    op0=ALU.mult, op1=ALU.subtract).then_inc(s_hlo, 1)

            def input_part(s, e, first):
                dve.wait_ge(s_tanh, s * (E * NG) + e * NG + 2)
                if first:
                    STT(out=C[:, e, :], in0=tmp[:, I, :], scalar=1.0, in1=tmp[:, G, :],
                        op0=ALU.add, op1=ALU.mult).then_inc(s_c, 1)
                    return
                STT(out=tmp[:, I, :], in0=tmp[:, I, :], scalar=1.0, in1=tmp[:, G, :],
                    op0=ALU.add, op1=ALU.mult).then_inc(s_u, 1)

            def cell(s, e):
                dve.wait_ge(s_tanh, s * (E * NG) + e * NG + 3)
                STT(out=tmp[:, F, :], in0=tmp[:, F, :], scalar=1.0, in1=C[:, e, :],
                    op0=ALU.add, op1=ALU.mult).then_inc(s_v, 1)
                dve.wait_ge(s_v, s * E + e - E + 1)
                dve.wait_ge(s_u, s * E + e - E + 1)
                STT(out=C[:, e, :], in0=tmp[:, F, :], scalar=0.5, in1=tmp[:, I, :],
                    op0=ALU.mult, op1=ALU.add).then_inc(s_c, 1)

            def add_y(s, e, k, par):
                y1 = s * (E * K) + e * K + k
                dve.wait_ge(s_y, y1 + 1)
                if e == 0 and k == 0:
                    dve.wait_ge(S["h2b"], s + 1)
                else:
                    dve.wait_ge(s_yadd, y1)
                for i in range(TILES):
                    last = STT(out=h2[:, par, i, :], in0=yp[:, i, :], scalar=wy[:, par, i, k, e:e + 1],
                               in1=h2[:, par, i, :], op0=ALU.mult, op1=ALU.add)
                last.then_inc(s_yadd, 1)

            def step(s, par, first, last):
                for t in range(NG * E):
                    e, g = t // NG, t % NG
                    if g == 0:
                        if e >= 3:
                            add_y(s, e - 3, 1, par)
                        elif not first:
                            add_y(s - 1, e - 3 + E, 1, 1 - par)
                    if g == 0 and e:
                        hidden(s, e - 1)
                    elif g == 0 and not first:
                        hidden(s - 1, E - 1)
                    if g == 1 and e < E - 1:
                        masked_input(s, e + 1, par, first and e == 0)
                    if g == 1 and e:
                        hidden_lo(s, e - 1)
                    elif g == 1 and not first:
                        hidden_lo(s - 1, E - 1)
                    if t == XM_AT and not last:
                        masked_input(s + 1, 0, 1 - par, False)
                    if g == 2:
                        if e >= 2:
                            add_y(s, e - 2, 0, par)
                        elif not first:
                            add_y(s - 1, e - 2 + E, 0, 1 - par)
                    if not last:
                        front(t, s + 1, 1 - par)
                    if g == 1:
                        input_part(s, e, first)
                    if g == 2 and not first:
                        cell(s, e)
            dve.wait_ge(s_zero, 1)
            for t in range(NG * E):
                front(t, 0, 0)
                if t == DVE_AT["moments"]:
                    split_w_lo(0, 4)
                if t == DVE_AT["w_max"]:
                    split_w_lo(4, 6)
                if t == DVE_AT["moments2"]:
                    split_w_lo(6, 7)
                    dve.wait_ge(s_wlo, 7)
                    V.memset(Hs[:, 0, 0, 0:2], 0.0).then_inc(s_wlo, 1)
            masked_input(0, 0, 0, True)
            run_steps(dve, step)
            hidden(STEPS - 1, E - 1)
            hidden_lo(STEPS - 1, E - 1)
            add_y(STEPS - 1, E - 3, 1, (STEPS - 1) % 2)
            for e in (E - 2, E - 1):
                for k in range(K):
                    add_y(STEPS - 1, e, k, (STEPS - 1) % 2)

        @block.gpsimd
        def _(pool):
            G_ = nc.gpsimd
            G_.memset(kf[:, 0:PAD], 0.0)
            G_.memset(kf[:, PAD + TF:], 0.0)
            G_.memset(vf[:, 0:PAD], 0.0)
            G_.memset(vf[:, PAD + TF:], 0.0)
            G_.memset(mhalf[:, :], -0.5)
            G_.memset(mones[:, :], -1.0)
            pool.wait_ge(s_dft, 2 * NSC)
            G_.memset(qbd[:, :], 0.0)
            pool.wait_ge(s_enc, 1)
            G_.memset(vz[:, :], 0.0).then_inc(s_zero, 1)

            def front(t, b):
                b1 = b + 1
                for at, ve, rs, mr, nm in (("moments", "veps", "rstd", "mr", "nmr"),
                                           ("moments2", "veps2", "rstd2", "mr2", "nmr2")):
                    if t == DVE_AT[at]:
                        pool.wait_ge(S[ve], b1)
                        G_.tensor_tensor(rstd[:, :], veps[:, :], mhalf[:, :], ALU.pow).then_inc(S[rs], 1)
                        pool.wait_ge(S[rs], b1)
                        G_.tensor_tensor(nmr[:, :], mv[:, :, 0], rstd[:, :], ALU.mult).then_inc(S[mr], 1)
                        pool.wait_ge(S[mr], b1)
                        G_.tensor_tensor(nmr[:, :], nmr[:, :], mones[:, :], ALU.mult).then_inc(S[nm], 1)

            def step(s, par, first, last):
                if not last:
                    for t in range(NG * E):
                        front(t, s + 1)

            pool.wait_ge(s_zero, 1)
            for t in range(NG * E):
                front(t, 0)
            run_steps(pool, step)


def kernel(**inputs):
    import numpy as np
    import concourse.bacc as bacc
    from concourse import mybir as mb
    from concourse.bass_utils import run_bass_kernel_spmd as run

    ids = np.ascontiguousarray(inputs["x"])
    STEPS, SEQ = ids.shape
    NFFT, VOCAB, ENC0, D_EMB, D = 64, 16, 32, 89, 128
    NFR, NFREQ, P, DH, PAD, QB, E = SEQ // NFFT + 1, NFFT // 2 + 1, 128, 16, 8, 16, 8
    pos = np.arange(NFR)[None, :] * NFFT + np.arange(NFFT)[:, None] - NFFT // 2
    pos = np.abs(pos)
    pos = np.where(pos > SEQ - 1, 2 * (SEQ - 1) - pos, pos)
    frames = np.ascontiguousarray(ids[:, pos].transpose(1, 0, 2).reshape(NFFT, STEPS * NFR))
    n = np.arange(NFFT)
    window = 0.5 - 0.5 * np.cos(2.0 * np.pi * n / NFFT)
    ang = 2.0 * np.pi * np.outer(n, np.arange(NFREQ)) / NFFT
    dft = np.stack([window[:, None] * np.cos(ang), window[:, None] * np.sin(ang)], axis=1).astype(np.float32)
    frame_rows = np.zeros((ENC0 + NFR, SEQ), np.float32)
    frame_rows[ENC0 + np.arange(SEQ) * NFR // SEQ, np.arange(SEQ)] = 1.0
    table = np.zeros((ENC0 + NFR, D), np.float32)
    table[:VOCAB, :D_EMB] = inputs["L0_tok_emb_table"]
    head = np.arange(P) // DH
    q, key = np.arange(P) % QB, np.arange(QB + 2 * PAD)
    inside = (key[None, :] >= q[:, None]) & (key[None, :] <= q[:, None] + 2 * PAD)
    data = {
        "x_ids": ids, "frame_ids": frames, "emb_table_padded": table,
        "proj_w": inputs["L0_tok_proj_w"], "proj_b": inputs["L0_tok_proj_b"],
        "w_qkv": inputs["L0_attn_W_qkv"], "b_qkv": np.asarray(inputs["L0_attn_b_qkv"]).reshape(3, P).T,
        "w_out": inputs["L0_attn_W_out"], "b_out": inputs["L0_attn_b_out"],
        "router_w": inputs["L0_ffn_router_w"], "router_b": inputs["L0_ffn_router_b"],
        "wi": inputs["L0_ffn_Wi"], "wh": inputs["L0_ffn_Wh"], "b_lstm": np.asarray(inputs["L0_ffn_b"]).reshape(E, 4, P).transpose(2, 0, 1),
        "wo": inputs["L0_ffn_Wo"], "bo": inputs["L0_ffn_bo"],
        "dft": dft,
        "vocab_col": np.arange(VOCAB, dtype=np.float32)[:, None],
        "vocab_rows": np.tile(np.arange(VOCAB, dtype=np.float32), (NFFT, 1)),
        "frame_rows": frame_rows,
        "ident": np.eye(P, dtype=np.float32),
        "head_ones": (head[:, None] == head[None, :]).astype(np.float32),
        "band": np.where(inside, 0.0, -1.0e30).astype(np.float32),
        "parity": (np.stack([head % 2 == 0, head % 2 == 1], axis=1) * 2.0 ** -12).astype(np.float32),
        "expert_m8": np.tile(np.arange(E, dtype=np.float32) - E, (P, 1)),
    }
    nc = bacc.Bacc("TRN2", target_bir_lowering=False, num_devices=1)
    arrays, args = {}, []
    for name, a in data.items():
        a = np.ascontiguousarray(a)
        arrays["in_" + name] = a
        args.append(nc.dram_tensor("in_" + name, a.shape, mb.dt.from_np(a.dtype), kind="ExternalInput").ap())
    args.append(nc.dram_tensor("out_dram", (STEPS, SEQ, D), mb.dt.float32, kind="ExternalOutput").ap())
    lm_tower_kernel(nc, *args)
    r = run(nc, [arrays], core_ids=[0])
    return r.results[0]["out_dram"]
```
